# Optimizing a Trainium2 kernel written in Bass

```python
import numpy as np
import jax
import jax.numpy as jnp

def _softmax(x, axis=-1):
    return jax.nn.softmax(x, axis=axis)

def _gelu(x):
    return jax.nn.gelu(x, approximate=True)

def _silu(x):
    return jax.nn.silu(x)

def _sigmoid(x):
    return jax.nn.sigmoid(x)

def _layernorm(x, axis=-1, eps=1e-05):
    m = jnp.mean(x, axis=axis, keepdims=True)
    v = jnp.var(x, axis=axis, keepdims=True)
    return (x - m) / jnp.sqrt(v + eps)

def _scatter_add(tgt, idx, src, axis=0):
    return tgt.at[idx].add(src)

def _segment_sum(src, seg, n):
    return jax.ops.segment_sum(src, seg, n)
kernel_name = 'mk_decoder_preln_d1_seqx_r8_950019'

def setup_inputs(seed: int=0):
    np.random.seed(seed)
    _w = jnp.asarray

    def _rec_inputs():
        import jax
        import jax.numpy as jnp
        _rk = jax.random.key(seed)
        x = 7.22e-05 + 1 * jax.random.normal(jax.random.fold_in(_rk, 1), (64, 64, 128), jnp.float32)
        _lenS = 64 - jax.random.randint(jax.random.fold_in(_rk, 7), (64,), 0, max(1, 64 // 4) + 1, jnp.int32)
        _lenS2 = 64 - jax.random.randint(jax.random.fold_in(_rk, 8), (64,), 0, max(1, 64 // 4) + 1, jnp.int32)
        _ctx_1024P = jax.random.normal(jax.random.fold_in(_rk, 11), (64, 16, 128), jnp.float32)
        _ctx_1024c = jax.random.dirichlet(jax.random.fold_in(_rk, 511), 0.3 * jnp.ones((16,), jnp.float32), (64, 64))
        _ctx_1024t = jnp.einsum('bsk,bkd->bsd', _ctx_1024c, _ctx_1024P)
        _ctx_1024t = _ctx_1024t * jax.lax.rsqrt(jnp.mean(jnp.square(_ctx_1024t)) + 1e-12) * 0.953939
        ctx_1024 = 4.13588e-05 + 0.999923 * (_ctx_1024t + 0.3 * jax.random.normal(jax.random.fold_in(_rk, 611), (64, 64, 128), jnp.float32))
        return (x, ctx_1024)
    x, ctx_1024 = _rec_inputs()

    def _L0_attn_setup():
        import jax, jax.numpy as jnp
        import numpy as np
        B, S, E, H, Dh = (2, 256, 128, 16, 64)
        key = jax.random.key(seed)
        ks = jax.random.split(key, 8)
        w = 0.02
        return {'x': jax.random.normal(ks[0], (B, S, E), jnp.float32), 'Wq': jax.random.normal(ks[1], (H, Dh, E), jnp.float32) * w, 'bq': jax.random.normal(ks[2], (H, Dh), jnp.float32) * w, 'Wk': jax.random.normal(ks[3], (H, Dh, E), jnp.float32) * w, 'bk': jax.random.normal(ks[4], (H, Dh), jnp.float32) * w, 'Wv': jax.random.normal(ks[5], (H, Dh, E), jnp.float32) * w, 'bv': jax.random.normal(ks[6], (H, Dh), jnp.float32) * w, 'proj': jax.random.normal(ks[7], (H * Dh, E), jnp.float32) * w}
    _L0_attn_all = _L0_attn_setup()
    _L0_attn_in = {k: v for k, v in _L0_attn_all.items() if k in ('Wq', 'bq', 'Wk', 'bk', 'Wv', 'bv', 'proj')}
    del _L0_attn_all

    def _L0_xattn_setup():
        import jax, jax.numpy as jnp
        import numpy as np
        DIM = 128
        NHEADS = 16
        HEAD_DIM = DIM // NHEADS
        SCALE = HEAD_DIM ** (-0.5)
        B, N = (4, 256)
        key = jax.random.key(seed)
        ks = jax.random.split(key, 11)
        s = 1.0 / np.sqrt(DIM)
        inp = {'query': jax.random.normal(ks[0], (B, N, DIM), jnp.float32), 'key': jax.random.normal(ks[1], (B, N, DIM), jnp.float32), 'value': jax.random.normal(ks[2], (B, N, DIM), jnp.float32), 'Wq': jax.random.normal(ks[3], (DIM, DIM), jnp.float32) * s, 'bq': jnp.zeros((DIM,), jnp.float32), 'Wk': jax.random.normal(ks[4], (DIM, DIM), jnp.float32) * s, 'bk': jnp.zeros((DIM,), jnp.float32), 'Wv': jax.random.normal(ks[5], (DIM, DIM), jnp.float32) * s, 'bv': jnp.zeros((DIM,), jnp.float32), 'Wo': jax.random.normal(ks[6], (DIM, DIM), jnp.float32) * s, 'bo': jnp.zeros((DIM,), jnp.float32)}
        return inp
    _L0_xattn_all = _L0_xattn_setup()
    _L0_xattn_in = {k: v for k, v in _L0_xattn_all.items() if k in ('Wq', 'bq', 'Wk', 'bk', 'Wv', 'bv', 'Wo', 'bo')}
    del _L0_xattn_all

    def _L0_ffn_setup():
        import jax, jax.numpy as jnp
        import numpy as np
        B, S, H = (1, 256, 128)
        E = 16
        I = 96
        TOPK = 4
        G = 4
        TOPK_G = 2
        SCALE = 2.5
        N_SHARED = 1

        def _route(x, gate_w, gate_bias):
            n = x.shape[0]
            logits = jnp.einsum('nh,eh->ne', x.astype(jnp.float32), gate_w)
            scores = jax.nn.sigmoid(logits)
            sb = scores + gate_bias
            gs = sb.reshape(n, G, E // G)
            group_scores = jnp.sum(jax.lax.top_k(gs, 2)[0], axis=-1)
            _, gidx = jax.lax.top_k(group_scores, TOPK_G)
            gmask = jnp.sum(jax.nn.one_hot(gidx, G, dtype=sb.dtype), axis=1)
            emask = jnp.repeat(gmask, E // G, axis=-1)
            masked = jnp.where(emask > 0, sb, -jnp.inf)
            _, tidx = jax.lax.top_k(masked, TOPK)
            w = jnp.take_along_axis(scores, tidx, axis=1)
            w = w / (jnp.sum(w, axis=-1, keepdims=True) + 1e-20)
            return (tidx, w * SCALE)
        key = jax.random.key(seed)
        ks = jax.random.split(key, 9)

        def rn(k, shape, scale=0.02):
            return jax.random.normal(k, shape, dtype=jnp.float32) * scale
        return dict(hidden_states=jax.random.normal(ks[0], (B, S, H), dtype=jnp.float32), gate_w=rn(ks[1], (E, H)), gate_bias=jax.random.normal(ks[2], (E,), dtype=jnp.float32) * 0.1, w1=rn(ks[3], (E, I, H)), w2=rn(ks[4], (E, H, I)), w3=rn(ks[5], (E, I, H)), ws1=rn(ks[6], (I * N_SHARED, H)), ws2=rn(ks[7], (H, I * N_SHARED)), ws3=rn(ks[8], (I * N_SHARED, H)))
    _L0_ffn_all = _L0_ffn_setup()
    _L0_ffn_in = {k: v for k, v in _L0_ffn_all.items() if k in ('gate_w', 'gate_bias', 'w1', 'w2', 'w3', 'ws1', 'ws2', 'ws3')}
    del _L0_ffn_all
    return {'x': x, 'ctx_1024': ctx_1024, 'L0_attn_Wq': _L0_attn_in['Wq'], 'L0_attn_bq': _L0_attn_in['bq'], 'L0_attn_Wk': _L0_attn_in['Wk'], 'L0_attn_bk': _L0_attn_in['bk'], 'L0_attn_Wv': _L0_attn_in['Wv'], 'L0_attn_bv': _L0_attn_in['bv'], 'L0_attn_proj': _L0_attn_in['proj'], 'L0_xattn_Wq': _L0_xattn_in['Wq'], 'L0_xattn_bq': _L0_xattn_in['bq'], 'L0_xattn_Wk': _L0_xattn_in['Wk'], 'L0_xattn_bk': _L0_xattn_in['bk'], 'L0_xattn_Wv': _L0_xattn_in['Wv'], 'L0_xattn_bv': _L0_xattn_in['bv'], 'L0_xattn_Wo': _L0_xattn_in['Wo'], 'L0_xattn_bo': _L0_xattn_in['bo'], 'L0_ffn_gate_w': _L0_ffn_in['gate_w'], 'L0_ffn_gate_bias': _L0_ffn_in['gate_bias'], 'L0_ffn_w1': _L0_ffn_in['w1'], 'L0_ffn_w2': _L0_ffn_in['w2'], 'L0_ffn_w3': _L0_ffn_in['w3'], 'L0_ffn_ws1': _L0_ffn_in['ws1'], 'L0_ffn_ws2': _L0_ffn_in['ws2'], 'L0_ffn_ws3': _L0_ffn_in['ws3']}

def reference(x, ctx_1024, L0_attn_Wq, L0_attn_bq, L0_attn_Wk, L0_attn_bk, L0_attn_Wv, L0_attn_bv, L0_attn_proj, L0_xattn_Wq, L0_xattn_bq, L0_xattn_Wk, L0_xattn_bk, L0_xattn_Wv, L0_xattn_bv, L0_xattn_Wo, L0_xattn_bo, L0_ffn_gate_w, L0_ffn_gate_bias, L0_ffn_w1, L0_ffn_w2, L0_ffn_w3, L0_ffn_ws1, L0_ffn_ws2, L0_ffn_ws3):
    import jax
    import jax.numpy as jnp

    def _L0_attn_ref(x, Wq, bq, Wk, bk, Wv, bv, proj):
        import jax, jax.numpy as jnp
        import numpy as np
        B, S, E, H, Dh = (2, 256, 128, 16, 64)
        b, s, e = x.shape
        h, dh, _ = Wq.shape
        scale = jnp.sqrt(jnp.asarray(dh, x.dtype))
        q = jnp.einsum('bse,hde->bhsd', x, Wq) + bq[None, :, None, :]
        k = jnp.einsum('bse,hde->bhsd', x, Wk) + bk[None, :, None, :]
        v = jnp.einsum('bse,hde->bhsd', x, Wv) + bv[None, :, None, :]
        causal = jnp.triu(jnp.ones((s, s), bool), 1)
        scores = jnp.einsum('bhsd,bhtd->bhst', q, k) / scale
        scores = jnp.where(causal[None, None], -jnp.inf, scores)
        att = jax.nn.softmax(scores, axis=-1) / scale
        z = jnp.einsum('bhst,bhtd->bhsd', att, v)
        z = z.reshape(b, s, h * dh)
        return z @ proj

    def _L0_xattn_ref(query, key, value, Wq, bq, Wk, bk, Wv, bv, Wo, bo):
        import jax, jax.numpy as jnp
        import numpy as np
        DIM = 128
        NHEADS = 16
        HEAD_DIM = DIM // NHEADS
        SCALE = HEAD_DIM ** (-0.5)
        B, N = (4, 256)
        b, n, c = query.shape
        q = query @ Wq.T + bq
        k = key @ Wk.T + bk
        v = value @ Wv.T + bv

        def split_heads(t):
            return t.reshape(b, -1, NHEADS, HEAD_DIM).transpose(0, 2, 1, 3).reshape(b * NHEADS, -1, HEAD_DIM)
        q, k, v = (split_heads(q), split_heads(k), split_heads(v))
        attn = jax.nn.softmax(jnp.einsum('bnd,bmd->bnm', q, k) * SCALE, axis=-1)
        x = jnp.einsum('bnm,bmd->bnd', attn, v).reshape(b, n, c)
        x = x @ Wo.T + bo
        return x

    def _L0_ffn_ref(hidden_states, gate_w, gate_bias, w1, w2, w3, ws1, ws2, ws3):
        import jax, jax.numpy as jnp
        import numpy as np
        B, S, H = (1, 256, 128)
        E = 16
        I = 96
        TOPK = 4
        G = 4
        TOPK_G = 2
        SCALE = 2.5
        N_SHARED = 1

        def _route(x, gate_w, gate_bias):
            n = x.shape[0]
            logits = jnp.einsum('nh,eh->ne', x.astype(jnp.float32), gate_w)
            scores = jax.nn.sigmoid(logits)
            sb = scores + gate_bias
            gs = sb.reshape(n, G, E // G)
            group_scores = jnp.sum(jax.lax.top_k(gs, 2)[0], axis=-1)
            _, gidx = jax.lax.top_k(group_scores, TOPK_G)
            gmask = jnp.sum(jax.nn.one_hot(gidx, G, dtype=sb.dtype), axis=1)
            emask = jnp.repeat(gmask, E // G, axis=-1)
            masked = jnp.where(emask > 0, sb, -jnp.inf)
            _, tidx = jax.lax.top_k(masked, TOPK)
            w = jnp.take_along_axis(scores, tidx, axis=1)
            w = w / (jnp.sum(w, axis=-1, keepdims=True) + 1e-20)
            return (tidx, w * SCALE)
        b, s, h = hidden_states.shape
        x = hidden_states.reshape(-1, h)
        tidx, tw = _route(x, gate_w, gate_bias)
        n = x.shape[0]
        combine = jnp.zeros((n, E), x.dtype).at[jnp.arange(n)[:, None], tidx].add(tw)
        g = jnp.einsum('nh,eih->nei', x, w1)
        u = jnp.einsum('nh,eih->nei', x, w3)
        hact = jax.nn.silu(g) * u * combine[:, :, None]
        y = jnp.einsum('nei,ehi->nh', hact, w2)
        shared = jnp.einsum('ni,hi->nh', jax.nn.silu(x @ ws1.T) * (x @ ws3.T), ws2)
        return (y + shared).reshape(b, s, h)
    x = x + _L0_attn_ref(_layernorm(x, axis=-1), L0_attn_Wq, L0_attn_bq, L0_attn_Wk, L0_attn_bk, L0_attn_Wv, L0_attn_bv, L0_attn_proj)
    x = x + _L0_xattn_ref(_layernorm(x, axis=-1), ctx_1024, ctx_1024, L0_xattn_Wq, L0_xattn_bq, L0_xattn_Wk, L0_xattn_bk, L0_xattn_Wv, L0_xattn_bv, L0_xattn_Wo, L0_xattn_bo)
    x = x + _L0_ffn_ref(_layernorm(x, axis=-1), L0_ffn_gate_w, L0_ffn_gate_bias, L0_ffn_w1, L0_ffn_w2, L0_ffn_w3, L0_ffn_ws1, L0_ffn_ws2, L0_ffn_ws3)
    return x

_drawn_inputs = setup_inputs


def setup_inputs(seed=0):
    import zlib

    import numpy as np

    out = dict(_drawn_inputs(seed))
    spreads = {'L0_xattn_bq': (0.0, 0.354),
     'L0_xattn_bk': (0.0, 0.8),
     'L0_xattn_bv': (0.0, 0.1),
     'L0_xattn_bo': (0.0, 0.1)}
    factors = {'L0_attn_Wq': 8.0,
     'L0_attn_bq': 8.0,
     'L0_attn_Wk': 8.0,
     'L0_attn_bk': 8.0,
     'L0_attn_Wv': 8.0,
     'L0_attn_bv': 8.0,
     'L0_attn_proj': 8.0,
     'L0_ffn_gate_w': 8.0,
     'L0_ffn_gate_bias': 8.0,
     'L0_ffn_w1': 8.0,
     'L0_ffn_w2': 8.0,
     'L0_ffn_w3': 8.0,
     'L0_ffn_ws1': 8.0,
     'L0_ffn_ws2': 8.0,
     'L0_ffn_ws3': 8.0}
    for name, (base, spread) in spreads.items():
        noise = np.random.default_rng([zlib.crc32(name.encode()), seed]).standard_normal(out[name].shape)
        drawn = base * np.exp(spread * noise) if base else spread * noise
        out[name] = jnp.asarray(drawn.astype(out[name].dtype))
    for name, factor in factors.items():
        out[name] = (out[name] * factor).astype(out[name].dtype)
    return out
```

```python
from contextlib import ExitStack

import concourse.bass as bass
from concourse import mybir

F32 = mybir.dt.float32
F32R = mybir.dt.float32r
BF16 = mybir.dt.bfloat16
ALU = mybir.AluOpType
ACT = mybir.ActivationFunctionType
AX_X = mybir.AxisListType.X

P = 128
E = 128
SEQ = 64
TOKENS = 64 * SEQ
NPAIR = 2
NB = 2 * NPAIR
TG = NPAIR * P
GROUPS = TOKENS // TG
H = 16
DH = 64
NJ = H // 2
DC = E // H
NU = 2 * NPAIR
JU = NJ // 2
HU = H // 2
NE, NI = 16, 96
FR = NE * NI
NC = FR // P + 1
NCB = (NC - 1) // 2
NQKV = NJ + NB
NR, NA = H, SEQ // H
NR2 = NR // 2
NG, EG = 4, NE // 4
EPS = 1e-5
NEG = -1e30
CW = 96

CH_LN, CH_A, CH_B, CH_R = 1, 3 * NU, 3 * NU, 24


ORDER = """
    a_ln.0 b_o.0-2 c_cb.3-3 c_cb.4-3 a_norm.0 b_t.3-2 c_cb.5-3 a_xT.0 c_gu.0-3 b_pv.3-2 b_write.1-2
    c_gu.1-3 a_qk.0 a_qk.1 c_gu.2-3 a_qk.2 a_qk.3 a_qk.4 a_qk.5 a_qk.6 a_qk.7 a_v.0 a_v.1 c_dn.0-3
    c_gu.3-3 b_back.1-2 c_dn.1-3 a_v.2 c_gu.4-3 c_dn.2-3 c_gu.5-3 a_v.3 c_dn.3-3 c_gu.6-3 b_zt.1-2
    c_dn.4-3 b_o.1-2 b_ln.0-1 c_gu.7-3 c_dn.5-3 a_s.0 a_s.1 b_norm.0-1 c_gu.8-3 c_dn.6-3 a_t.0 c_gu.9-3
    b_xT.0-1 c_dn.7-3 a_pv.0 c_gu.10-3 b_qk.0-1 c_dn.8-3 a_zt.0 a_s.2 b_v.0-1 a_t.1 b_kbd.0-1 c_gu.11-3
    b_kbd.1-1 c_dn.9-3 c_gu.12-3 b_s.0-1 c_dn.10-3 a_pv.1 c_dn.11-3 c_dn.12-3 c_out.0-3 a_zt.1 c_ln.0-2
    b_s.1-1 c_norm.0-2 b_t.0-1 a_pr.0 c_xT.0-2 a_s.3 b_pv.0-1 a_t.2 b_s.2-1 c_lg.0-2 b_t.1-1 a_pv.2
    c_route.0-2 a_zt.2 c_route.1-2 b_pv.1-1 b_write.0-1 a_t.3 b_back.0-1 b_s.3-1 a_pv.3 c_route.2-2
    c_route.3-2 b_t.2-1 a_zt.3 b_pv.2-1 a_pr.1 c_ct.0-2 c_cb.0-2 b_zt.0-1 c_cb.1-2 c_cb.2-2
"""
LAG = 3


def schedule():
    out = []
    for word in ORDER.split():
        name, _, behind = word.partition("-")
        step, number = name.split(".")
        out.append((step, int(number), int(behind or 0)))
    return out


def decoder_layer(nc, x, x_hba, ctx_in, w_qk, w_v, w_proj, b_qk, b_v, wc_qkvo, bc_qk, bc_vo,
                  gate_w, gate_b, w13, w2, c_ident, c_mask, c_head, c_sel, c_lower, out):
    with ExitStack() as stack:
        def sb(name, shape, dt=F32):
            return stack.enter_context(nc.sbuf_tensor(name, shape, dt))

        def sem(name):
            return stack.enter_context(nc.semaphore(name))

        def bank(name):
            return stack.enter_context(nc.psum_tensor(name, [P, 512], F32))

        SA = [bank("SA0"), bank("SA1")]
        XA = bank("XA")
        SB, XB = bank("SB"), bank("XB")
        GU = [bank("GU0"), bank("GU1")]
        Y = bank("Y")
        RING = [SA[0], SA[1], XA]

        wqk_hi, wqk_lo = sb("wqk_hi", [P, 2, NJ * P], F32R), sb("wqk_lo", [P, 2, NJ * P], F32R)
        wv = sb("wv", [P, 2, NJ * DH])
        wproj = sb("wproj", [P, NJ, E])
        bqk, bv = sb("bqk", [P, 2, NJ]), sb("bv", [P, NJ * DH])
        wc = sb("wc", [P, 4, E])
        bcqk, bcvo = sb("bcqk", [P, 2]), sb("bcvo", [P, 2, E])
        gw, gb = sb("gw", [P, NE]), sb("gb", [P, NE])
        w13_hi, w13_lo = sb("w13_hi", [P, 2, FR + NI], F32R), sb("w13_lo", [P, 2, FR + NI], F32R)
        w13_in = sb("w13_in", [P, 2, FR + NI])
        w2s = sb("w2s", [P, NC, E])
        ident, identb = sb("ident", [P, P]), sb("identb", [P, P], BF16)
        maskb = sb("maskb", [P, HU, SEQ], BF16)
        head = sb("head", [P, H])
        selb = sb("selb", [CW, NC - 1, P], BF16)
        lowerb = sb("lowerb", [P, NE, NE], BF16)
        half, gate = sb("half", [P, NPAIR]), sb("gate", [P, 1])

        xin, xres = sb("xin", [P, NPAIR, E]), sb("xres", [P, NPAIR, E])
        xh1, X1 = sb("xh1", [P, NPAIR, E]), sb("X1", [P, NPAIR, E])
        xT, xT_hi, xT_lo = sb("xT", [P, TG]), sb("xT_hi", [P, TG], F32R), sb("xT_lo", [P, TG], F32R)
        QT = sb("QT", [P, NJ, TG])
        KT = sb("KT", [P, NJ, NB, 2, SEQ])
        V = sb("V", [P, NB, NJ, 2, DH])
        DA = [sb("DA0", [P, 512]), sb("DA1", [P, 512])]
        PTA, zA, zT = sb("PTA", [P, 512]), sb("zA", [P, 512]), sb("zT", [P, NR2, NPAIR, H, 2 * NA])
        mxA, smA, rA = sb("mxA", [P, HU]), sb("smA", [P, HU]), sb("rA", [P, 2, HU])
        cin = sb("cin", [P, NPAIR, E])
        xh2, X1b, X2 = sb("xh2", [P, NPAIR, E]), sb("X1b", [P, NPAIR, E]), sb("X2", [P, NPAIR, E])
        xcT = sb("xcT", [P, 2, TG])
        QcT, KcT = sb("QcT", [P, TG]), sb("KcT", [P, TG])
        KBD = sb("KBD", [P, NPAIR, 2, H, SEQ])
        Vc = sb("Vc", [P, NB, NJ, 2, DC])
        DB = [sb("DB0", [P, 512]), sb("DB1", [P, 512])]
        PTB, zcT = sb("PTB", [P, 512]), sb("zcT", [P, P])
        zc, zr = sb("zc", [P, NPAIR, E]), sb("zr", [P, NPAIR, E])
        mxB, smB, rB = sb("mxB", [P, HU]), sb("smB", [P, HU]), sb("rB", [P, 2, HU])
        xh3, X2b, yo = sb("xh3", [P, NPAIR, E]), sb("X2b", [P, NPAIR, E]), sb("yo", [P, NPAIR, E])
        x3T, x3_hi, x3_lo = sb("x3T", [P, TG]), sb("x3_hi", [P, TG], F32R), sb("x3_lo", [P, TG], F32R)
        tl = sb("tl", [P, NPAIR, NE])
        scr, sbias, wsel = (sb(n, [P, NPAIR, NE]) for n in ("scr", "sbias", "wsel"))
        pmx, pmn = sb("pmx", [P, NPAIR * NG, 2]), sb("pmn", [P, NPAIR * NG, 2])
        gs, gcnt = sb("gs", [P, NPAIR, NG]), sb("gcnt", [P, NPAIR, NG])
        g_gt, g_eq = sb("g_gt", [P, NPAIR, NG, NG], BF16), sb("g_eq", [P, NPAIR, NG, NG], BF16)
        e_gt, e_eq = sb("e_gt", [P, NPAIR, NE, NE], BF16), sb("e_eq", [P, NPAIR, NE, NE], BF16)
        ecnt, wsum = sb("ecnt", [P, NPAIR, NE]), sb("wsum", [P, NPAIR])
        comb3 = sb("comb3", [P, NPAIR, CW], BF16)
        combT = sb("combT", [CW, TG], BF16)
        CB = sb("CB", [P, NC - 1, TG])
        HB = [sb(f"HB{n}", [P, TG]) for n in range(3)]
        st = [sb(f"st{k}", [P, NPAIR, 6]) for k in range(3)]
        mv = [sb(f"mv{k}", [P, NPAIR, 2]) for k in range(3)]
        ve = [sb(f"ve{k}", [P, NPAIR]) for k in range(3)]
        rs = [sb(f"rs{k}", [P, NPAIR]) for k in range(3)]

        s_w = sem("s_w"); s_w13 = sem("s_w13"); s_wrest = sem("s_wrest")
        s_xin = sem("s_xin"); s_xres = sem("s_xres"); s_ctx = sem("s_ctx"); s_out = sem("s_out")
        act_w = sem("act_w"); dve_w = sem("dve_w"); pool_w = sem("pool_w")
        act_w13 = sem("act_w13"); dve_w13 = sem("dve_w13")
        ln_st = [sem(f"ln_st{k}") for k in range(3)]
        ln_mv = [sem(f"ln_mv{k}") for k in range(3)]
        ln_ve = [sem(f"ln_ve{k}") for k in range(3)]
        ln_rs = [sem(f"ln_rs{k}") for k in range(3)]
        ln_xh = [sem(f"ln_xh{k}") for k in range(3)]
        pe_axT = sem("pe_axT"); act_axT = sem("act_axT"); dve_axlo = sem("dve_axlo")
        pe_qkv = sem("pe_qkv"); act_k = sem("act_k"); act_q = sem("act_q"); dve_k = sem("dve_k")
        dve_v = sem("dve_v")
        pe_as = sem("pe_as"); dve_amx = sem("dve_amx"); dve_asub = sem("dve_asub"); act_ae = sem("act_ae")
        dve_asm = sem("dve_asm"); dve_ar = sem("dve_ar")
        pe_at = sem("pe_at"); act_apt = sem("act_apt"); pe_apv = sem("pe_apv"); dve_az = sem("dve_az")
        pe_azt = sem("pe_azt"); act_azt = sem("act_azt"); pe_apr = sem("pe_apr"); dve_x1 = sem("dve_x1")
        dve_x1b = sem("dve_x1b")
        pe_bxT = sem("pe_bxT"); act_bxT = sem("act_bxT"); pe_bqk = sem("pe_bqk"); act_bqk = sem("act_bqk")
        pe_bv = sem("pe_bv"); dve_bv = sem("dve_bv"); pool_kbd = sem("pool_kbd")
        pe_bs = sem("pe_bs"); dve_bmx = sem("dve_bmx"); dve_bsub = sem("dve_bsub"); act_be = sem("act_be")
        dve_bsm = sem("dve_bsm"); dve_br = sem("dve_br")
        pe_bt = sem("pe_bt"); act_bpt = sem("act_bpt"); pe_bpv = sem("pe_bpv"); dve_bz = sem("dve_bz")
        pe_bzt = sem("pe_bzt"); act_bzt = sem("act_bzt"); pe_bo = sem("pe_bo"); dve_x2 = sem("dve_x2")
        dve_x2b = sem("dve_x2b")
        pe_cxT = sem("pe_cxT"); act_cxT = sem("act_cxT"); dve_cxlo = sem("dve_cxlo")
        pe_lg = sem("pe_lg"); dve_route_chain = sem("dve_route_chain"); dve_part = sem("dve_part"); act_tl = sem("act_tl"); dve_route = sem("dve_route"); dve_comb = sem("dve_comb")
        pe_ct = sem("pe_ct"); act_ct = sem("act_ct"); pe_cb = sem("pe_cb"); act_cb = sem("act_cb")
        pe_gu = sem("pe_gu"); act_gu = sem("act_gu"); dve_p1 = sem("dve_p1"); dve_p2 = sem("dve_p2")
        pool_h = sem("pool_h"); pe_dn = sem("pe_dn"); dve_out = sem("dve_out")

        s_zw = sem("s_zw"); s_zr = sem("s_zr")
        N_W, N_WREST = 12, 3

        z_dram = nc.dram_tensor("z_dram", [NPAIR, H, P, DC], F32, kind="Internal").ap()
        x_g = x.rearrange("(g t p) e -> g p t e", t=NPAIR, p=P)
        ctx_g = ctx_in.rearrange("(g t p) e -> g p t e", t=NPAIR, p=P)
        xr_g = x_hba.rearrange("(g t p) e -> g p t e", t=NPAIR, p=P)
        out_g = out.rearrange("(g t p) e -> g p t e", t=NPAIR, p=P)

        def due(count):
            return not isinstance(count, int) or count > 0

        def run(eng, walk):
            def once(i):
                for step, n, behind in schedule():
                    if not isinstance(i, int) or 0 <= i - behind < GROUPS:
                        walk(step, n, i - behind)

            for i in range(LAG + 1):
                once(i)
            with eng.Fori(LAG + 1, GROUPS) as i:
                once(i)
            for i in range(GROUPS, GROUPS + LAG):
                once(i)

        block = stack.enter_context(nc.Block())

        @block.sync
        def _(sp):
            sp.dma_start(xin[:], x_g[0]).then_inc(s_xin, 16)
            for dst, src in ((V[:].rearrange("p b j h d -> p (b j h d)")[:, 0:2 * NJ * P], w_qk),
                             (ident[:], c_ident), (bqk[:].rearrange("p a j -> p (a j)"), b_qk),
                             (wv[:].rearrange("p a n -> p (a n)"), w_v), (bv[:], b_v),
                             (KT[:].rearrange("p j b h k -> p (j b h k)")[:, 0:HU * SEQ], c_mask),
                             (wproj[:].rearrange("p j e -> p (j e)"), w_proj),
                             (wc[:].rearrange("p a e -> p (a e)"), wc_qkvo), (bcqk[:], bc_qk),
                             (bcvo[:].rearrange("p a e -> p (a e)"), bc_vo), (head[:], c_head),
                             (KT[:].rearrange("p j b h k -> p (j b h k)")[:, 512:512 + NE * NE], c_lower)):
                sp.dma_start(dst, src).then_inc(s_w, 16)
            sp.dma_start(w13_in[:].rearrange("p a n -> p (a n)"), w13).then_inc(s_w13, 16)
            sp.dma_start(CB[:].rearrange("p c t -> p (c t)")[0:CW, 0:(NC - 1) * P], c_sel).then_inc(s_w13, 16)
            for dst, src in ((gw[:], gate_w), (gb[:], gate_b), (w2s[:].rearrange("p c e -> p (c e)"), w2)):
                sp.dma_start(dst, src).then_inc(s_wrest, 16)

            def a_ln(n, g):
                if due(g):
                    sp.wait_ge(ln_xh[0], g)
                    sp.dma_start(xin[:], x_g[g]).then_inc(s_xin, 16)

            def b_ln(n, g):
                if due(g):
                    sp.wait_ge(pe_bxT, g)
                sp.dma_start(cin[:], ctx_g[g]).then_inc(s_ctx, 16)

            def a_s(u, g):
                if u == 0:
                    if due(NPAIR * g):
                        sp.wait_ge(dve_x1, NPAIR * g)
                    sp.dma_start(xres[:], xr_g[g]).then_inc(s_xres, 16)

            does = {"a_ln": a_ln, "a_s": a_s, "b_ln": b_ln}

            def walk(step, n, g):
                if step in does:
                    does[step](n, g)

            run(sp, walk)

        @block.tensor
        def _(pe):
            mm, tr = nc.tensor.matmul, nc.tensor.transpose

            def split_product(o, w_hi, w_lo, x_hi, x_lo):
                mm(o, w_hi, x_hi, start=True, stop=False)
                mm(o, w_lo, x_hi, start=False, stop=False)
                return mm(o, w_hi, x_lo, start=False, stop=True)

            def a_xT(n, g):
                pe.wait_ge(ln_xh[0], g + 1)
                if due(NPAIR * g):
                    pe.wait_ge(dve_x1, NPAIR * g)
                for t in range(NPAIR):
                    last = tr(XA[:, t * P:(t + 1) * P], xh1[:, t, :], ident[:])
                last.then_inc(pe_axT, 1)

            def a_qk(j, g):
                if j == 0:
                    pe.wait_ge(act_axT, 2 * (g + 1))
                    pe.wait_ge(dve_axlo, g + 1)
                    if due(NU * g):
                        pe.wait_ge(dve_asub, NU * g)
                if j >= 3:
                    pe.wait_ge(act_q, NJ * g + j - 2)
                b = RING[j % 3]
                cols = slice(j * P, (j + 1) * P)
                split_product(b[:, 0:TG], wqk_hi[:, 0, cols], wqk_lo[:, 0, cols], xT_hi[:], xT_lo[:])
                split_product(b[:, TG:2 * TG], wqk_hi[:, 1, cols], wqk_lo[:, 1, cols],
                              xT_hi[:], xT_lo[:]).then_inc(pe_qkv, 1)

            def a_v(b, g):
                n = NJ + b
                if n - 3 < NJ:
                    pe.wait_ge(act_q, NJ * g + n - 2)
                else:
                    pe.wait_ge(dve_v, 2 * NB * g + 2 * (n - 2 - NJ))
                for h2 in range(2):
                    last = mm(RING[n % 3][64 * h2:64 * h2 + 64, :], xT[:, b * SEQ:(b + 1) * SEQ],
                              wv[:, h2, :], start=True, stop=True)
                last.then_inc(pe_qkv, 1)

            def a_s(u, g):
                p, hf = u // 2, u % 2
                if u == 0:
                    pe.wait_ge(act_k, NJ * (g + 1))
                    pe.wait_ge(act_q, NJ * (g + 1))
                    pe.wait_ge(dve_k, NJ * (g + 1))
                if u < 2:
                    pe.wait_ge(dve_v, 2 * NB * g + 2 * (u + 2))
                else:
                    if due(NU * g + u - 1):
                        pe.wait_ge(dve_asub, NU * g + u - 1)
                S = SA[u % 2]
                mm(S[:], identb[:], maskb[:].rearrange("p h k -> p (h k)"), start=True, stop=False,
                   skip_group_check=True)
                for jj in range(JU):
                    for b2 in range(2):
                        b = 2 * p + b2
                        last = mm(S[64 * b2:64 * b2 + 64, jj * P:(jj + 1) * P],
                                  QT[:, JU * hf + jj, b * SEQ:(b + 1) * SEQ],
                                  KT[:, JU * hf + jj, b, :, :].rearrange("p h k -> p (h k)"),
                                  start=False, stop=True, skip_group_check=True)
                last.then_inc(pe_as, 1)

            def a_t(u, g):
                pe.wait_ge(act_ae, NU * g + u + 1)
                if u == 0:
                    pe.wait_ge(dve_v, 2 * NB * (g + 1))
                elif u % 2:
                    if due(NU * g + u):
                        pe.wait_ge(act_azt, NU * g + u)
                else:
                    if due(NPAIR * g + u // 2):
                        pe.wait_ge(dve_x1, NPAIR * g + u // 2)
                for jj in range(JU):
                    last = tr(XA[:, jj * P:(jj + 1) * P], DA[u % 2][:, jj * P:(jj + 1) * P], ident[:])
                last.then_inc(pe_at, 1)

            def a_pv(u, g):
                p, hf = u // 2, u % 2
                pe.wait_ge(act_apt, NU * g + u + 1)
                for jj in range(JU):
                    for b2 in range(2):
                        last = mm(XA[64 * b2:64 * b2 + 64, jj * P:(jj + 1) * P],
                                  PTA[:, jj * P + 64 * b2:jj * P + 64 * b2 + 64],
                                  V[:, 2 * p + b2, JU * hf + jj, :, :].rearrange("p h d -> p (h d)"),
                                  start=True, stop=True)
                last.then_inc(pe_apv, 1)

            def a_zt(u, g):
                pe.wait_ge(dve_az, NU * g + u + 1)
                for jj in range(JU):
                    last = tr(XA[:, jj * P:(jj + 1) * P], zA[:, jj * P:(jj + 1) * P], ident[:])
                last.then_inc(pe_azt, 1)

            def a_pr(p, g):
                pe.wait_ge(act_azt, NU * g + 2 * p + 2)
                for r in range(NR2):
                    last = mm(XA[:, 0:E], zT[:, r, p, :, :].rearrange("p h c -> p (h c)"),
                              wproj[:, r, :], start=(r == 0), stop=(r == NR2 - 1))
                last.then_inc(pe_apr, 1)

            def b_xT(n, g):
                pe.wait_ge(ln_xh[1], g + 1)
                pe.wait_ge(s_ctx, 16 * (g + 1))
                if due(NPAIR * g):
                    pe.wait_ge(dve_x2, NPAIR * g)
                for t in range(NPAIR):
                    tr(XB[:, t * P:(t + 1) * P], xh2[:, t, :], ident[:])
                for t in range(NPAIR):
                    last = tr(XB[:, TG + t * P:TG + (t + 1) * P], cin[:, t, :], ident[:])
                last.then_inc(pe_bxT, 1)

            def b_qk(n, g):
                pe.wait_ge(act_bxT, g + 1)
                if due(NU * g):
                    pe.wait_ge(dve_bsub, NU * g)
                for a in range(2):
                    last = mm(SB[:, a * TG:(a + 1) * TG], wc[:, a, :], xcT[:, a, :], start=True, stop=True)
                last.then_inc(pe_bqk, 1)

            def b_v(n, g):
                pe.wait_ge(act_bxT, g + 1)
                for b in range(NB):
                    for h2 in range(2):
                        last = mm(XB[64 * h2:64 * h2 + 64, b * E:(b + 1) * E],
                                  xcT[:, 1, b * SEQ:(b + 1) * SEQ], wc[:, 2, :], start=True, stop=True)
                last.then_inc(pe_bv, 1)

            def b_s(u, g):
                p, hf = u // 2, u % 2
                pe.wait_ge(pool_kbd, NB * g + 2 * p + 2)
                if u == 0:
                    pe.wait_ge(act_bqk, 2 * (g + 1))
                else:
                    if due(NU * g + u):
                        pe.wait_ge(dve_bsub, NU * g + u)
                for b2 in range(2):
                    b = 2 * p + b2
                    last = mm(SB[64 * b2:64 * b2 + 64, :], QcT[:, b * SEQ:(b + 1) * SEQ],
                              KBD[:, p, b2, HU * hf:HU * (hf + 1), :].rearrange("p h k -> p (h k)"),
                              start=True, stop=True)
                last.then_inc(pe_bs, 1)

            def b_t(u, g):
                pe.wait_ge(act_be, NU * g + u + 1)
                if u == 0:
                    pe.wait_ge(dve_bv, 2 * (g + 1))
                elif u < 3:
                    if due(NU * g + u):
                        pe.wait_ge(dve_bz, NU * g + u)
                else:
                    pe.wait_ge(dve_x2, NPAIR * g + 1)
                for jj in range(JU):
                    last = tr(XB[:, jj * P:(jj + 1) * P], DB[u % 2][:, jj * P:(jj + 1) * P], ident[:])
                last.then_inc(pe_bt, 1)

            def b_pv(u, g):
                p, hf = u // 2, u % 2
                pe.wait_ge(act_bpt, NU * g + u + 1)
                for jj in range(JU):
                    for b2 in range(2):
                        v = Vc[:, 2 * p + b2, :, :, :].rearrange("p j h d -> p (j h d)")
                        last = mm(XB[64 * b2:64 * b2 + 64, jj * CW:(jj + 1) * CW],
                                  PTB[:, jj * P + 64 * b2:jj * P + 64 * b2 + 64],
                                  v[:, (E - CW) * hf:(E - CW) * hf + CW], start=True, stop=True)
                last.then_inc(pe_bpv, 1)

            def b_zt(p, g):
                if due(16 * (NPAIR * g + p + 1)):
                    pe.wait_ge(s_zr, 16 * (NPAIR * g + p + 1))
                pe.wait_ge(dve_bz, NU * g + 3 + p)
                tr(XB[:, 0:P], zr[:, p, :], ident[:]).then_inc(pe_bzt, 1)

            def b_o(p, g):
                pe.wait_ge(act_bzt, NPAIR * g + p + 1)
                mm(XB[:, 0:E], zcT[:], wc[:, 3, :], start=True, stop=True).then_inc(pe_bo, 1)

            def c_xT(n, g):
                pe.wait_ge(ln_xh[2], g + 1)
                if due(g):
                    pe.wait_ge(dve_out, g)
                for t in range(NPAIR):
                    last = tr(Y[:, t * P:(t + 1) * P], xh3[:, t, :], ident[:])
                last.then_inc(pe_cxT, 1)

            def c_lg(n, g):
                pe.wait_ge(act_cxT, 2 * (g + 1))
                if due(NC * g):
                    pe.wait_ge(dve_p2, NC * g)
                for t in range(NPAIR):
                    last = mm(GU[0][:, t * NE:(t + 1) * NE], x3T[:, t * P:(t + 1) * P], gw[:],
                              start=True, stop=True)
                last.then_inc(pe_lg, 1)

            def c_ct(n, g):
                pe.wait_ge(dve_comb, g + 1)
                o = GU[1][:].bitcast(BF16)
                for t in range(NPAIR):
                    last = tr(o[0:CW, t * P:(t + 1) * P], comb3[:, t, :], identb[:])
                last.then_inc(pe_ct, 1)

            def c_cb(k, g):
                if k == 0:
                    pe.wait_ge(act_ct, g + 1)
                    pe.wait_ge(act_tl, g + 1)
                elif k >= 2:
                    pe.wait_ge(act_cb, NCB * g + k - 1)
                for a in range(2):
                    last = mm(GU[k % 2][:, a * TG:(a + 1) * TG], selb[:, 2 * k + a, :], combT[:],
                              start=True, stop=True)
                last.then_inc(pe_cb, 1)

            def c_gu(c, g):
                if c == 0:
                    pe.wait_ge(dve_cxlo, g + 1)
                if c < 2:
                    pe.wait_ge(act_cb, NCB * g + NCB - 1 + c)
                else:
                    pe.wait_ge(dve_p2, NC * g + c - 1)
                m = P if c < NC - 1 else NI
                cols = slice(c * P, c * P + m)
                for a in range(2):
                    last = split_product(GU[c % 2][0:m, a * TG:(a + 1) * TG], w13_hi[:, a, cols],
                                         w13_lo[:, a, cols], x3_hi[:], x3_lo[:])
                last.then_inc(pe_gu, 1)

            def c_dn(c, g):
                m = P if c < NC - 1 else NI
                if c < NC - 1:
                    pe.wait_ge(pool_h, (NC - 1) * g + c + 1)
                else:
                    pe.wait_ge(dve_p2, NC * (g + 1))
                for t in range(NPAIR):
                    last = mm(Y[:, t * E:(t + 1) * E], HB[c % 3][0:m, t * P:(t + 1) * P],
                              w2s[0:m, c, :], start=(c == 0 and t == 0), stop=(c == NC - 1),
                              skip_group_check=True)
                last.then_inc(pe_dn, 1)

            does = {"a_xT": a_xT, "a_qk": a_qk, "a_v": a_v, "a_s": a_s, "a_t": a_t, "a_pv": a_pv,
                    "a_zt": a_zt, "a_pr": a_pr, "b_xT": b_xT, "b_qk": b_qk, "b_v": b_v, "b_s": b_s,
                    "b_t": b_t, "b_pv": b_pv, "b_zt": b_zt, "b_o": b_o, "c_xT": c_xT, "c_lg": c_lg,
                    "c_ct": c_ct, "c_cb": c_cb, "c_gu": c_gu, "c_dn": c_dn}

            def walk(step, n, g):
                if step == "b_ln" and isinstance(g, int) and g == 0:
                    weights_13()
                if step in does:
                    does[step](n, g)

            def weights_13():
                pe.wait_ge(act_w13, 2)
                pe.wait_ge(dve_w13, 1)
                pe.wait_ge(s_wrest, 16 * N_WREST)

            pe.wait_ge(s_w, 16 * N_W)
            pe.wait_ge(act_w, 4)
            pe.wait_ge(dve_w, 1)
            pe.wait_ge(pool_w, 4)
            run(pe, walk)

        @block.scalar
        def _(act):
            func, copy = nc.scalar.activation, nc.scalar.copy

            def a_xT(n, g):
                act.wait_ge(pe_axT, g + 1)
                copy(xT[:], XA[:, 0:TG]).then_inc(act_axT, 1)
                copy(xT_hi[:], XA[:, 0:TG]).then_inc(act_axT, 1)

            def a_qk(j, g):
                b = RING[j % 3]
                act.wait_ge(pe_qkv, NQKV * g + j + 1)
                func(KT[0:64, j, :, 0, :], b[0:64, TG:2 * TG].rearrange("p (b k) -> p b k", k=SEQ),
                     ACT.Identity, bias=bqk[0:64, 1, j:j + 1]).then_inc(act_k, 1)
                act.wait_ge(dve_k, NJ * g + j + 1)
                func(QT[:, j, :], b[:, 0:TG], ACT.Identity, bias=bqk[:, 0, j:j + 1]).then_inc(act_q, 1)

            def a_s(u, g):
                act.wait_ge(dve_asub, NU * g + u + 1)
                func(DA[u % 2][:], DA[u % 2][:], ACT.Exp, scale=DH ** -0.5).then_inc(act_ae, 1)

            def a_t(u, g):
                act.wait_ge(pe_at, NU * g + u + 1)
                copy(PTA[:], XA[:]).then_inc(act_apt, 1)

            def a_zt(u, g):
                p, hf = u // 2, u % 2
                act.wait_ge(pe_azt, NU * g + u + 1)
                for h2 in range(2):
                    src = XA[64 * h2:64 * h2 + 64, :].rearrange("p (j c r s) -> p s r j c", j=JU, c=2 * NA, s=2)
                    for r2 in range(2):
                        last = copy(zT[64 * r2:64 * r2 + 64, :, p, HU * hf + h2:HU * (hf + 1):2, :],
                                    src[:, r2, :, :, :])
                last.then_inc(act_azt, 1)

            def b_xT(n, g):
                act.wait_ge(pe_bxT, g + 1)
                for t in range(NPAIR):
                    copy(xcT[:, 0, t * P:(t + 1) * P].rearrange("p (b h a) -> p b h a", b=2, h=H),
                         XB[:, t * P:(t + 1) * P].rearrange("p (h b a) -> p b h a", b=2, h=H))
                copy(xcT[:, 1, :], XB[:, TG:2 * TG]).then_inc(act_bxT, 1)

            def b_qk(n, g):
                act.wait_ge(pe_bqk, g + 1)
                if due(NB * g):
                    act.wait_ge(pool_kbd, NB * g)
                for a, dst in enumerate((QcT, KcT)):
                    func(dst[:], SB[:, a * TG:(a + 1) * TG], ACT.Identity,
                         bias=bcqk[:, a:a + 1]).then_inc(act_bqk, 1)

            def b_s(u, g):
                act.wait_ge(dve_bsub, NU * g + u + 1)
                func(DB[u % 2][:], DB[u % 2][:], ACT.Exp, scale=DC ** -0.5).then_inc(act_be, 1)

            def b_t(u, g):
                act.wait_ge(pe_bt, NU * g + u + 1)
                copy(PTB[:], XB[:]).then_inc(act_bpt, 1)

            def b_write(p, g):
                act.wait_ge(dve_bz, NU * g + 2 * p + 2)
                if due(NPAIR * (g - 1) + p + 1):
                    act.wait_ge(pe_bzt, NPAIR * (g - 1) + p + 1)
                act.dma_start(z_dram[p].rearrange("h q d -> q h d"),
                              zc[:, p, :].rearrange("q (h d) -> q h d", d=DC)).then_inc(s_zw, 16)

            def b_back(p, g):
                if due(16 * (NPAIR * g + p + 1)):
                    act.wait_ge(s_zw, 16 * (NPAIR * g + p + 1))
                act.dma_start(zr[:, p, :], z_dram[p].rearrange("h (c r) d -> (h c) (r d)", r=NR))\
                    .then_inc(s_zr, 16)

            def b_zt(p, g):
                act.wait_ge(pe_bzt, NPAIR * g + p + 1)
                copy(zcT[:], XB[:, 0:P]).then_inc(act_bzt, 1)

            def c_xT(n, g):
                act.wait_ge(pe_cxT, g + 1)
                copy(x3T[:], Y[:, 0:TG]).then_inc(act_cxT, 1)
                copy(x3_hi[:], Y[:, 0:TG]).then_inc(act_cxT, 1)

            def c_lg(n, g):
                act.wait_ge(pe_lg, g + 1)
                if due(g):
                    act.wait_ge(dve_route, g)
                func(tl[:].rearrange("p t e -> p (t e)"), GU[0][:, 0:NPAIR * NE], ACT.Tanh,
                     scale=0.5).then_inc(act_tl, 1)

            def c_ct(n, g):
                act.wait_ge(pe_ct, g + 1)
                copy(combT[:], GU[1][:].bitcast(BF16)[0:CW, 0:TG]).then_inc(act_ct, 1)

            def c_cb(k, g):
                act.wait_ge(pe_cb, NCB * g + k + 1)
                if due((NC - 1) * (g - 1) + 2 * k + 2):
                    act.wait_ge(pool_h, (NC - 1) * (g - 1) + 2 * k + 2)
                copy(CB[:, 2 * k:2 * k + 2, :].rearrange("p c t -> p (c t)"),
                     GU[k % 2][:]).then_inc(act_cb, 1)

            def c_gu(c, g):
                m = P if c < NC - 1 else NI
                act.wait_ge(pe_gu, NC * g + c + 1)
                if due(NC * g + c - 2):
                    act.wait_ge(pe_dn, NC * g + c - 2)
                func(HB[c % 3][0:m, :], GU[c % 2][0:m, 0:TG], ACT.Tanh, scale=0.5).then_inc(act_gu, 1)

            def c_out(n, g):
                act.wait_ge(dve_out, g + 1)
                act.dma_start(out_g[g], yo[:]).then_inc(s_out, 16)

            does = {"a_xT": a_xT, "a_qk": a_qk, "a_s": a_s, "a_t": a_t, "a_zt": a_zt, "b_xT": b_xT,
                    "b_qk": b_qk, "b_s": b_s, "b_t": b_t, "b_zt": b_zt, "b_write": b_write, "b_back": b_back, "c_xT": c_xT, "c_lg": c_lg,
                    "c_ct": c_ct, "c_cb": c_cb, "c_gu": c_gu, "c_out": c_out}

            def walk(step, n, g):
                if step == "b_ln" and isinstance(g, int) and g == 0:
                    weights_13()
                if step in does:
                    does[step](n, g)

            def weights_13():
                act.wait_ge(s_w13, 32)
                copy(w13_hi[:], w13_in[:]).then_inc(act_w13, 1)
                copy(selb[:].rearrange("p c m -> p (c m)"),
                     CB[:].rearrange("p c t -> p (c t)")[0:CW, 0:(NC - 1) * P]).then_inc(act_w13, 1)

            act.wait_ge(s_w, 16 * N_W)
            copy(wqk_hi[:].rearrange("p a n -> p (a n)"),
                 V[:].rearrange("p b j h d -> p (b j h d)")[:, 0:2 * NJ * P]).then_inc(act_w, 1)
            copy(identb[:], ident[:]).then_inc(act_w, 1)
            copy(maskb[:].rearrange("p h k -> p (h k)"),
                 KT[:].rearrange("p j b h k -> p (j b h k)")[:, 0:HU * SEQ]).then_inc(act_w, 1)
            copy(lowerb[:].rearrange("p e f -> p (e f)"),
                 KT[:].rearrange("p j b h k -> p (j b h k)")[:, 512:512 + NE * NE]).then_inc(act_w, 1)
            run(act, walk)
            act.wait_ge(s_out, 16 * GROUPS)

        @block.vector
        def _(dve):
            tt, ts, stt, red = (nc.vector.tensor_tensor, nc.vector.tensor_scalar,
                                nc.vector.scalar_tensor_tensor, nc.vector.tensor_reduce)

            def ln(k, src, g):
                for t in range(NPAIR):
                    last = nc.vector.bn_stats(st[k][:, t, :], src[:, t, :])
                last.then_inc(ln_st[k], 1)
                dve.wait_ge(ln_st[k], g + 1)
                nc.vector.memset(gate[:], 0.0)
                for t in range(NPAIR):
                    last = nc.vector.bn_aggr(mv[k][:, t, :], st[k][:, t, :])
                last.then_inc(ln_mv[k], 1)
                dve.wait_ge(ln_mv[k], g + 1)
                ts(ve[k][:], mv[k][:, :, 1], EPS, None, ALU.add).then_inc(ln_ve[k], 1)

            def norm(k, src, dst, g):
                dve.wait_ge(ln_rs[k], g + 1)
                for t in range(NPAIR):
                    last = ts(dst[:, t, :], src[:, t, :], mv[k][:, t, 0:1], rs[k][:, t:t + 1],
                              ALU.subtract, ALU.mult)
                last.then_inc(ln_xh[k], 1)

            def a_ln(n, g):
                dve.wait_ge(s_xin, 16 * (g + 1))
                ln(0, xin, g)

            def a_norm(n, g):
                if due(g):
                    dve.wait_ge(pe_axT, g)
                norm(0, xin, xh1, g)

            def a_xT(n, g):
                dve.wait_ge(act_axT, 2 * (g + 1))
                tt(xT_lo[:], XA[:, 0:TG], xT_hi[:].bitcast(F32), ALU.subtract).then_inc(dve_axlo, 1)

            def a_qk(j, g):
                dve.wait_ge(pe_qkv, NQKV * g + j + 1)
                ts(KT[64:128, j, :, 1, :],
                   RING[j % 3][64:128, TG:2 * TG].rearrange("p (b k) -> p b k", k=SEQ),
                   bqk[64:128, 1, j:j + 1], None, ALU.add).then_inc(dve_k, 1)

            def a_v(b, g):
                dve.wait_ge(pe_qkv, NQKV * g + NJ + b + 1)
                for h2 in range(2):
                    half_p = slice(64 * h2, 64 * h2 + 64)
                    tt(V[half_p, b, :, h2, :],
                       RING[(NJ + b) % 3][half_p, :].rearrange("p (j d) -> p j d", d=DH),
                       bv[half_p, :].rearrange("p (j d) -> p j d", d=DH), ALU.add).then_inc(dve_v, 1)

            def softmax_shift(u, g, S, D, mx, pe_s, s_mx, s_sub, pe_t):
                dve.wait_ge(pe_s, NU * g + u + 1)
                if due(NU * g + u):
                    dve.wait_ge(s_sub, NU * g + u)
                red(mx[:], S[:].rearrange("p (h k) -> p h k", k=SEQ), AX_X, ALU.max).then_inc(s_mx, 1)
                dve.wait_ge(s_mx, NU * g + u + 1)
                if due(NU * g + u - 1):
                    dve.wait_ge(pe_t, NU * g + u - 1)
                tt(D[u % 2][:].rearrange("p (h k) -> p h k", k=SEQ),
                   S[:].rearrange("p (h k) -> p h k", k=SEQ),
                   mx[:].unsqueeze(2).to_broadcast([P, HU, SEQ]), ALU.subtract).then_inc(s_sub, 1)

            def softmax_sum(u, g, D, sm, r, act_e, s_sm, s_r):
                dve.wait_ge(act_e, NU * g + u + 1)
                if due(NU * g + u):
                    dve.wait_ge(s_r, NU * g + u)
                red(sm[:], D[u % 2][:].rearrange("p (h k) -> p h k", k=SEQ), AX_X, ALU.add)\
                    .then_inc(s_sm, 1)
                dve.wait_ge(s_sm, NU * g + u + 1)
                nc.vector.reciprocal(r[:, u % 2, :], sm[:]).then_inc(s_r, 1)

            def a_s(u, g):
                softmax_shift(u, g, SA[u % 2], DA, mxA, pe_as, dve_amx, dve_asub, pe_at)

            def a_t(u, g):
                softmax_sum(u, g, DA, smA, rA, act_ae, dve_asm, dve_ar)

            def a_pv(u, g):
                dve.wait_ge(pe_apv, NU * g + u + 1)
                dve.wait_ge(dve_ar, NU * g + u + 1)
                if due(NU * g + u):
                    dve.wait_ge(pe_azt, NU * g + u)
                tt(zA[:].rearrange("p (h d) -> p h d", d=DH), XA[:].rearrange("p (h d) -> p h d", d=DH),
                   rA[:, u % 2, :].unsqueeze(2).to_broadcast([P, HU, DH]), ALU.mult).then_inc(dve_az, 1)

            def a_pr(p, g):
                dve.wait_ge(pe_apr, NPAIR * g + p + 1)
                if p == 0:
                    dve.wait_ge(s_xres, 16 * (g + 1))
                    if due(g):
                        dve.wait_ge(dve_x1b, g)
                    if due(g):
                        dve.wait_ge(ln_xh[1], g)
                stt(X1[:, p, :], XA[:, 0:E], DH ** -0.5, xres[:, p, :], ALU.mult, ALU.add)\
                    .then_inc(dve_x1, 1)

            def b_ln(n, g):
                dve.wait_ge(dve_x1, NPAIR * (g + 1))
                ln(1, X1, g)
                if due(NPAIR * g):
                    dve.wait_ge(dve_x2, NPAIR * g)
                tt(X1b[:], X1[:], bcvo[:, 1, :].unsqueeze(1).to_broadcast([P, NPAIR, E]), ALU.add)\
                    .then_inc(dve_x1b, 1)

            def b_norm(n, g):
                if due(g):
                    dve.wait_ge(pe_bxT, g)
                norm(1, X1, xh2, g)

            def b_v(n, g):
                dve.wait_ge(pe_bv, g + 1)
                for h2 in range(2):
                    half_p = slice(64 * h2, 64 * h2 + 64)
                    tt(Vc[half_p, :, :, h2, :].rearrange("p b j d -> p b j d"),
                       XB[half_p, :].rearrange("p (b j h d) -> p b j h d", b=NB, j=NJ, h=2)[:, :, :, h2, :],
                       bcvo[half_p, 0, :].rearrange("p (j h d) -> p j h d", j=NJ, h=2)[:, :, h2, :]
                       .unsqueeze(1).to_broadcast([64, NB, NJ, DC]), ALU.add).then_inc(dve_bv, 1)

            def b_s(u, g):
                softmax_shift(u, g, SB, DB, mxB, pe_bs, dve_bmx, dve_bsub, pe_bt)

            def b_t(u, g):
                softmax_sum(u, g, DB, smB, rB, act_be, dve_bsm, dve_br)

            def b_pv(u, g):
                p, hf = u // 2, u % 2
                dve.wait_ge(pe_bpv, NU * g + u + 1)
                dve.wait_ge(dve_br, NU * g + u + 1)
                if due(16 * (NPAIR * (g - 1) + p + 1)):
                    dve.wait_ge(s_zw, 16 * (NPAIR * (g - 1) + p + 1))
                own = XB[:, (E - CW) * hf:(E - CW) * hf + JU * (CW + 2 * DC)]
                own = own.rearrange("p (j c) -> p j c", j=JU)[:, :, 0:2 * DC]
                tt(zc[:, p, 64 * hf:64 * hf + 64].rearrange("p (j h d) -> p j h d", j=JU, h=2),
                   own.rearrange("p j (h d) -> p j h d", h=2),
                   rB[:, u % 2, :].rearrange("p (j h) -> p j h", h=2).unsqueeze(3)
                   .to_broadcast([P, JU, 2, DC]), ALU.mult).then_inc(dve_bz, 1)

            def b_o(p, g):
                dve.wait_ge(pe_bo, NPAIR * g + p + 1)
                if p == 0:
                    dve.wait_ge(dve_x1b, g + 1)
                    if due(g):
                        dve.wait_ge(dve_x2b, g)
                    if due(g):
                        dve.wait_ge(ln_xh[2], g)
                tt(X2[:, p, :], XB[:, 0:E], X1b[:, p, :], ALU.add).then_inc(dve_x2, 1)

            def c_ln(n, g):
                dve.wait_ge(dve_x2, NPAIR * (g + 1))
                ln(2, X2, g)
                if due(g):
                    dve.wait_ge(dve_out, g)
                nc.vector.tensor_copy(X2b[:], X2[:]).then_inc(dve_x2b, 1)

            def c_norm(n, g):
                if due(g):
                    dve.wait_ge(pe_cxT, g)
                norm(2, X2, xh3, g)

            def c_xT(n, g):
                dve.wait_ge(act_cxT, 2 * (g + 1))
                tt(x3_lo[:], Y[:, 0:TG], x3_hi[:].bitcast(F32), ALU.subtract).then_inc(dve_cxlo, 1)

            def c_route(part, g):
                first = [0, 8, 13, 18][part]
                done = [first]

                def link(ins):
                    done[0] += 1
                    ins.then_inc(dve_route_chain, 1)
                    dve.wait_ge(dve_route_chain, CH_R * g + done[0])

                if part == 0:
                    dve.wait_ge(act_tl, g + 1)
                    link(ts(scr[:], tl[:], 0.5, 0.5, ALU.mult, ALU.add))
                    link(tt(sbias[:], scr[:], gb[:].unsqueeze(1).to_broadcast([P, NPAIR, NE]), ALU.add))
                    pairs = sbias[:].rearrange("p t (g a b) -> p (t g) a b", a=2, b=2)
                    link(tt(pmx[:], pairs[:, :, :, 0], pairs[:, :, :, 1], ALU.max))
                    link(tt(pmn[:], pairs[:, :, :, 0], pairs[:, :, :, 1], ALU.min))
                    gs_f = gs[:].rearrange("p t g -> p (t g)")
                    link(tt(pmn[:], pmx[:], pmn[:], ALU.add))
                    link(tt(gs_f, pmx[:, :, 0], pmx[:, :, 1], ALU.add))
                    link(tt(gs_f, gs_f, pmn[:, :, 0], ALU.max))
                    link(tt(gs_f, gs_f, pmn[:, :, 1], ALU.max))
                elif part == 1:
                    other = gs[:].unsqueeze(2).to_broadcast([P, NPAIR, NG, NG])
                    own = gs[:].unsqueeze(3).to_broadcast([P, NPAIR, NG, NG])
                    lower = lowerb[:, 0:NG, 0:NG].unsqueeze(1).to_broadcast([P, NPAIR, NG, NG])
                    tt(g_gt[:], other, own, ALU.is_gt)
                    link(tt(g_eq[:], other, own, ALU.is_equal))
                    link(tt(g_eq[:], g_eq[:], lower, ALU.mult))
                    link(tt(g_gt[:], g_gt[:], g_eq[:], ALU.add))
                    link(red(gcnt[:], g_gt[:], AX_X, ALU.add))
                    link(ts(gcnt[:], gcnt[:], 1.5, NEG, ALU.is_gt, ALU.mult))
                elif part == 2:
                    by_group = gcnt[:].rearrange("p t g -> p (t g)").unsqueeze(2)
                    flat = sbias[:].rearrange("p t (g e) -> p (t g) e", e=EG)
                    link(tt(flat, flat, by_group.to_broadcast([P, NPAIR * NG, EG]), ALU.add))
                    other = sbias[:].unsqueeze(2).to_broadcast([P, NPAIR, NE, NE])
                    own = sbias[:].unsqueeze(3).to_broadcast([P, NPAIR, NE, NE])
                    lower = lowerb[:].unsqueeze(1).to_broadcast([P, NPAIR, NE, NE])
                    tt(e_gt[:], other, own, ALU.is_gt)
                    link(tt(e_eq[:], other, own, ALU.is_equal))
                    link(tt(e_eq[:], e_eq[:], lower, ALU.mult))
                    link(tt(e_gt[:], e_gt[:], e_eq[:], ALU.add))
                    link(red(ecnt[:], e_gt[:], AX_X, ALU.add))
                else:
                    if due(g):
                        dve.wait_ge(pe_ct, g)
                    link(stt(wsel[:], ecnt[:], 3.5, scr[:], ALU.is_lt, ALU.mult))
                    link(red(wsum[:], wsel[:], AX_X, ALU.add))
                    link(ts(wsum[:], wsum[:], 1e-20, None, ALU.add))
                    link(nc.vector.reciprocal(wsum[:], wsum[:]))
                    link(tt(wsel[:], wsel[:], wsum[:].unsqueeze(2).to_broadcast([P, NPAIR, NE]), ALU.mult))
                    link(ts(wsel[:], wsel[:], 2.5, None, ALU.mult))
                    nc.vector.tensor_copy(comb3[:, :, 0:NE], wsel[:]).then_inc(dve_route, 1)
                    dve.wait_ge(dve_route, g + 1)
                    tt(wsel[:], wsel[:], comb3[:, :, 0:NE], ALU.subtract).then_inc(dve_part, 1)
                    dve.wait_ge(dve_part, 3 * g + 1)
                    nc.vector.tensor_copy(comb3[:, :, 32:32 + NE], wsel[:]).then_inc(dve_part, 1)
                    dve.wait_ge(dve_part, 3 * g + 2)
                    tt(wsel[:], wsel[:], comb3[:, :, 32:32 + NE], ALU.subtract).then_inc(dve_part, 1)
                    dve.wait_ge(dve_part, 3 * g + 3)
                    nc.vector.tensor_copy(comb3[:, :, 64:64 + NE], wsel[:]).then_inc(dve_comb, 1)

            def c_gu(c, g):
                m = P if c < NC - 1 else NI
                hb = HB[c % 3][0:m, :]
                dve.wait_ge(act_gu, NC * g + c + 1)
                stt(hb, hb, 1.0, GU[c % 2][0:m, 0:TG], ALU.add, ALU.mult).then_inc(dve_p1, 1)
                dve.wait_ge(dve_p1, NC * g + c + 1)
                stt(hb, GU[c % 2][0:m, TG:2 * TG], 0.5, hb, ALU.mult, ALU.mult).then_inc(dve_p2, 1)

            def c_out(n, g):
                dve.wait_ge(pe_dn, NC * (g + 1))
                dve.wait_ge(dve_x2b, g + 1)
                if due(16 * g):
                    dve.wait_ge(s_out, 16 * g)
                tt(yo[:].rearrange("p t e -> p (t e)"), Y[:, 0:TG],
                   X2b[:].rearrange("p t e -> p (t e)"), ALU.add).then_inc(dve_out, 1)

            does = {"a_ln": a_ln, "a_norm": a_norm, "a_xT": a_xT, "a_qk": a_qk, "a_v": a_v, "a_s": a_s,
                    "a_t": a_t, "a_pv": a_pv, "a_pr": a_pr, "b_ln": b_ln, "b_norm": b_norm, "b_v": b_v,
                    "b_s": b_s, "b_t": b_t, "b_pv": b_pv, "b_o": b_o, "c_ln": c_ln, "c_norm": c_norm,
                    "c_xT": c_xT, "c_route": c_route, "c_gu": c_gu, "c_out": c_out}

            def walk(step, n, g):
                if step == "b_ln" and isinstance(g, int) and g == 0:
                    weights_13()
                if step in does:
                    does[step](n, g)

            def weights_13():
                dve.wait_ge(act_w13, 1)
                tt(w13_lo[:], w13_in[:], w13_hi[:].bitcast(F32), ALU.subtract).then_inc(dve_w13, 1)
                dve.wait_ge(s_wrest, 16 * N_WREST)

            dve.wait_ge(act_w, 1)
            tt(wqk_lo[:].rearrange("p a n -> p (a n)"),
               V[:].rearrange("p b j h d -> p (b j h d)")[:, 0:2 * NJ * P],
               wqk_hi[:].rearrange("p a n -> p (a n)").bitcast(F32), ALU.subtract).then_inc(dve_w, 1)
            dve.wait_ge(s_w, 16 * N_W)
            dve.wait_ge(act_w, 4)
            dve.wait_ge(pool_w, 5)
            run(dve, walk)

        @block.gpsimd
        def _(pool):
            def power(k, g):
                pool.wait_ge(ln_ve[k], g + 1)
                if due(g):
                    pool.wait_ge(ln_xh[k], g)
                nc.gpsimd.tensor_tensor(rs[k][:], ve[k][:], half[:], ALU.pow).then_inc(ln_rs[k], 1)

            def b_kbd(p, g):
                pool.wait_ge(act_bqk, 2 * (g + 1))
                if due(NU * (g - 1) + 2 * p + 2):
                    pool.wait_ge(pe_bs, NU * (g - 1) + 2 * p + 2)
                for b2 in range(2):
                    b = 2 * p + b2
                    nc.gpsimd.tensor_tensor(
                        KBD[:, p, b2, :, :],
                        KcT[:, b * SEQ:(b + 1) * SEQ].unsqueeze(1).to_broadcast([P, H, SEQ]),
                        head[:].unsqueeze(2).to_broadcast([P, H, SEQ]), ALU.mult).then_inc(pool_kbd, 1)

            def c_gu(c, g):
                if c < NC - 1:
                    pool.wait_ge(dve_p2, NC * g + c + 1)
                    pool.wait_ge(act_cb, NCB * g + c // 2 + 1)
                    nc.gpsimd.tensor_tensor(HB[c % 3][:], HB[c % 3][:], CB[:, c, :], ALU.mult)\
                        .then_inc(pool_h, 1)

            does = {"a_ln": lambda n, g: power(0, g), "b_ln": lambda n, g: power(1, g),
                    "c_ln": lambda n, g: power(2, g), "b_kbd": b_kbd, "c_gu": c_gu}

            def walk(step, n, g):
                if step in does:
                    does[step](n, g)

            nc.gpsimd.memset(half[:], -0.5).then_inc(pool_w, 1)
            nc.gpsimd.memset(Vc[:], 0.0).then_inc(pool_w, 1)
            pool.wait_ge(dve_w, 1)
            pool.wait_ge(act_w, 4)
            nc.gpsimd.memset(V[:], 0.0).then_inc(pool_w, 1)
            nc.gpsimd.memset(KT[:], 0.0).then_inc(pool_w, 1)
            nc.gpsimd.memset(comb3[:], 0.0).then_inc(pool_w, 1)
            pool.wait_ge(pool_w, 5)
            pool.wait_ge(s_w, 16 * N_W)
            run(pool, walk)


def kernel(**inputs):
    import numpy as np
    import concourse.bacc as bacc
    from concourse import mybir as mb
    from concourse.bass_utils import run_bass_kernel_spmd

    a = {k: np.asarray(v) for k, v in inputs.items()}

    def heads_t(w):
        return w.reshape(H * DH, E).T

    def by_parity(w):
        return w.reshape(NJ, 2, DH, -1).transpose(3, 1, 0, 2)

    def columns(b):
        return b.reshape(NJ, P).T

    def rows(b, n=P):
        return np.tile(b.reshape(1, -1), (n, 1))

    bv2 = a["L0_attn_bv"].reshape(NJ, 2, DH).transpose(1, 0, 2).reshape(2, NJ * DH)
    w1 = np.concatenate([a["L0_ffn_w1"].reshape(FR, E), a["L0_ffn_ws1"]], 0).T
    w3 = np.concatenate([a["L0_ffn_w3"].reshape(FR, E), a["L0_ffn_ws3"]], 0).T
    w2 = np.zeros((NC * P, E), np.float32)
    w2[0:FR] = a["L0_ffn_w2"].transpose(0, 2, 1).reshape(FR, E)
    w2[FR:FR + NI] = a["L0_ffn_ws2"].T
    q = np.arange(P) % SEQ
    mask = np.where(np.arange(SEQ)[None, :] > q[:, None], np.float32(NEG), np.float32(0))
    sel = np.zeros((CW, (NC - 1) * P), np.float32)
    for part in range(3):
        sel[32 * part + np.arange(FR) // NI, np.arange(FR)] = 1
    given = [
        ("x", a["x"].reshape(TOKENS, E)),
        ("x_hba", a["x"].reshape(TOKENS // P, 2, H, NA, E).transpose(0, 2, 1, 3, 4).reshape(TOKENS, E)),
        ("ctx", a["ctx_1024"].reshape(TOKENS, E)),
        ("w_qk", np.concatenate([heads_t(a["L0_attn_Wq"]), heads_t(a["L0_attn_Wk"])], 1)),
        ("w_v", by_parity(a["L0_attn_Wv"]).reshape(E, 2 * NJ * DH)),
        ("w_proj", a["L0_attn_proj"].reshape(NJ, P, E).transpose(1, 0, 2).reshape(P, NJ * E)),
        ("b_qk", np.concatenate([columns(a["L0_attn_bq"]), columns(a["L0_attn_bk"])], 1)),
        ("b_v", np.repeat(bv2, 64, 0)),
        ("wc_qkvo", np.concatenate([a["L0_xattn_" + n].T for n in ("Wq", "Wk", "Wv", "Wo")], 1)),
        ("bc_qk", np.stack([a["L0_xattn_bq"], a["L0_xattn_bk"]], 1)),
        ("bc_vo", rows(np.concatenate([a["L0_xattn_bv"], a["L0_xattn_bo"]]))),
        ("gate_w", a["L0_ffn_gate_w"].T), ("gate_b", rows(a["L0_ffn_gate_bias"])),
        ("w13", np.concatenate([w1, w3], 1)),
        ("w2", w2.reshape(NC, P, E).transpose(1, 0, 2).reshape(P, NC * E)),
        ("c_ident", np.eye(P, dtype=np.float32)), ("c_mask", np.tile(mask, (1, HU))),
        ("c_head", (np.arange(P)[:, None] // DC == np.arange(H)[None, :]).astype(np.float32)),
        ("c_sel", sel),
        ("c_lower", rows((np.arange(NE)[None, :] < np.arange(NE)[:, None]).astype(np.float32))),
    ]
    nc = bacc.Bacc("TRN2", target_bir_lowering=False, num_devices=1)
    arrays, args = {}, []
    for name, v in given:
        arrays["in_" + name] = np.ascontiguousarray(v)
        args.append(nc.dram_tensor("in_" + name, v.shape, mb.dt.from_np(v.dtype), kind="ExternalInput").ap())
    args.append(nc.dram_tensor("out_0", (TOKENS, E), mb.dt.float32, kind="ExternalOutput").ap())
    decoder_layer(nc, *args)
    r = run_bass_kernel_spmd(nc, [arrays], core_ids=[0])
    o = r.results[0]["out_0"].reshape(TOKENS // P, H, 2, NA, E).transpose(0, 2, 1, 3, 4)
    return np.ascontiguousarray(o).reshape(TOKENS // SEQ, SEQ, E)
```

```python
from contextlib import ExitStack

import concourse.bass as bass
from concourse import mybir

F32 = mybir.dt.float32
F32R = mybir.dt.float32r
BF16 = mybir.dt.bfloat16
ALU = mybir.AluOpType
ACT = mybir.ActivationFunctionType
AX_X = mybir.AxisListType.X

P = 128
E = 128
SEQ = 64
TOKENS = 64 * SEQ
NPAIR = 2
NB = 2 * NPAIR
TG = NPAIR * P
GROUPS = TOKENS // TG
H = 16
DH = 64
NJ = H // 2
DC = E // H
NU = 2 * NPAIR
JU = NJ // 2
HU = H // 2
NE, NI = 16, 96
FR = NE * NI
NC = FR // P + 1
NCB = (NC - 1) // 2
NQKV = NJ + NB
NR, NA = H, SEQ // H
NR2 = NR // 2
NG, EG = 4, NE // 4
EPS = 1e-5
NEG = -1e30
CW = 96

CH_R = 21


ORDER = """
    b_pv.2-2 a_ln.0 a_pr.1-1 c_ct.0-3 b_zt.0-2 c_cb.0-3 b_o.0-2 c_cb.1-3 c_cb.2-3 b_t.3-2 a_norm.0 a_xT.0
    c_cb.3-3 c_cb.4-3 b_pv.3-2 b_ln.0-1 a_qk.0 c_cb.5-3 b_write.1-2 a_qk.1 c_gu.0-3 c_gu.1-3 a_qk.2 a_qk.3
    c_gu.2-3 c_dn.0-3 a_qk.4 a_qk.5 b_back.1-2 a_qk.6 a_qk.7 c_gu.3-3 a_v.0 c_dn.1-3 c_gu.4-3 c_dn.2-3
    c_gu.5-3 b_norm.0-1 a_v.1 a_v.2 a_v.3 a_s.0 b_zt.1-2 c_dn.3-3 c_gu.6-3 c_dn.4-3 c_gu.7-3 a_s.1 b_o.1-2
    c_dn.5-3 c_gu.8-3 a_t.0 c_dn.6-3 c_gu.9-3 b_xT.0-1 c_dn.7-3 a_pv.0 c_gu.10-3 b_qk.0-1 a_zt.0 a_s.2
    b_v.0-1 a_t.1 c_dn.8-3 b_kbd.0-1 c_gu.11-3 c_dn.9-3 c_gu.12-3 b_kbd.1-1 b_s.0-1 a_pv.1 c_dn.10-3
    c_dn.11-3 c_dn.12-3 a_zt.1 c_out.0-3 c_ln.0-2 b_s.1-1 c_norm.0-2 b_t.0-1 a_pr.0 c_xT.0-2 a_s.3
    b_pv.0-1 a_t.2 c_lg.0-2 b_s.2-1 a_pv.2 b_t.1-1 c_route.0-2 c_route.1-2 a_zt.2 b_pv.1-1 b_write.0-1
    a_t.3 b_back.0-1 b_s.3-1 a_pv.3 b_t.2-1 c_route.2-2 a_zt.3 c_route.3-2
"""
LAG = 3


def schedule():
    out = []
    for word in ORDER.split():
        name, _, behind = word.partition("-")
        step, number = name.split(".")
        out.append((step, int(number), int(behind or 0)))
    return out


def decoder_layer(nc, x, x_hba, ctx_in, w_qk, w_v, w_proj, b_qk, b_v, wc_qkvo, bc_qk, bc_v, bc_o,
                  gate_w, gate_b, w13, w2, c_ident, c_mask, c_head, c_sel, c_lower, out):
    with ExitStack() as stack:
        def sb(name, shape, dt=F32):
            return stack.enter_context(nc.sbuf_tensor(name, shape, dt))

        def sem(name):
            return stack.enter_context(nc.semaphore(name))

        def bank(name):
            return stack.enter_context(nc.psum_tensor(name, [P, 512], F32))

        SA = [bank("SA0"), bank("SA1")]
        XA = bank("XA")
        SB, XB = bank("SB"), bank("XB")
        GU = [bank("GU0"), bank("GU1")]
        Y = bank("Y")
        RING = [SA[0], SA[1], XA]

        wqk_hi, wqk_lo = (sb(n, [P, 2, 2, JU, P], F32R) for n in ("wqk_hi", "wqk_lo"))
        wv = sb("wv", [P, 2, NJ * DH])
        wproj = sb("wproj", [P, NJ, E])
        bqk = sb("bqk", [P, 2, NJ])
        bv_t, bcv_t = sb("bv_t", [P, P]), sb("bcv_t", [P, P])
        bias_a, bias_b = sb("bias_a", [P, E]), sb("bias_b", [P, E])
        wc = sb("wc", [P, 4, E])
        bcqk, bo = sb("bcqk", [P, 2]), sb("bo", [P, E])
        gw, gb = sb("gw", [P, NE]), sb("gb", [P, NE])
        w13_hi, w13_lo = sb("w13_hi", [P, 2, FR + NI], F32R), sb("w13_lo", [P, 2, FR + NI], F32R)
        w13_in = sb("w13_in", [P, 2, FR + NI])
        w2s = sb("w2s", [P, NC, E])
        ident, identb = sb("ident", [P, P]), sb("identb", [P, P], BF16)
        maskb = sb("maskb", [P, HU, SEQ], BF16)
        head = sb("head", [P, H])
        selb = sb("selb", [CW, NC - 1, P], BF16)
        lowerb = sb("lowerb", [P, NE, NE], BF16)
        half, gate = sb("half", [P, NPAIR]), sb("gate", [P, 1])

        xin, xres = sb("xin", [P, NPAIR, E]), sb("xres", [P, NPAIR, E])
        xh1, X1 = sb("xh1", [P, NPAIR, E]), sb("X1", [P, NPAIR, E])
        xT, xT_hi, xT_lo = sb("xT", [P, TG]), sb("xT_hi", [P, TG], F32R), sb("xT_lo", [P, TG], F32R)
        QT = sb("QT", [P, NJ, TG])
        KT = sb("KT", [P, NJ, NB, 2, SEQ])
        V = sb("V", [P, NB, NJ, 2, DH])
        DA = [sb("DA0", [P, 512]), sb("DA1", [P, 512])]
        PTA, zA, zT = sb("PTA", [P, 512]), sb("zA", [P, 512]), sb("zT", [P, NR2, NPAIR, H, 2 * NA])
        mxA, smA, rA = sb("mxA", [P, HU]), sb("smA", [P, HU]), sb("rA", [P, 2, HU])
        cin = sb("cin", [P, NPAIR, E])
        xh2, X1b, X2 = sb("xh2", [P, NPAIR, E]), sb("X1b", [P, NPAIR, E]), sb("X2", [P, NPAIR, E])
        xcT = sb("xcT", [P, 2, TG])
        QcT, KcT = sb("QcT", [P, TG]), sb("KcT", [P, TG])
        KBD = sb("KBD", [P, NPAIR, 2, H, SEQ])
        Vc = sb("Vc", [P, NB, E + 4])
        DB = [sb("DB0", [P, 512]), sb("DB1", [P, 512])]
        PTB, zcT = sb("PTB", [P, 512]), sb("zcT", [P, P])
        zc, zr = sb("zc", [P, NPAIR, E]), sb("zr", [P, NPAIR, E])
        mxB, rB = sb("mxB", [P, HU]), sb("rB", [P, JU, 2])
        xh3, X2b, yo = sb("xh3", [P, NPAIR, E]), sb("X2b", [P, NPAIR, E]), sb("yo", [P, NPAIR, E])
        x3T, x3_hi, x3_lo = sb("x3T", [P, TG]), sb("x3_hi", [P, TG], F32R), sb("x3_lo", [P, TG], F32R)
        tl = sb("tl", [P, NPAIR, NE])
        scr, sbias, wsel = (sb(n, [P, NPAIR, NE]) for n in ("scr", "sbias", "wsel"))
        pmx, pmn = sb("pmx", [P, NPAIR * NG, 2]), sb("pmn", [P, NPAIR * NG, 2])
        gs, gcnt = sb("gs", [P, NPAIR, NG]), sb("gcnt", [P, NPAIR, NG])
        g_gt, g_eq = sb("g_gt", [P, NPAIR, NG, NG], BF16), sb("g_eq", [P, NPAIR, NG, NG], BF16)
        e_gt, e_eq = sb("e_gt", [P, NPAIR, NE, NE], BF16), sb("e_eq", [P, NPAIR, NE, NE], BF16)
        ecnt, wsum = sb("ecnt", [P, NPAIR, NE]), sb("wsum", [P, NPAIR])
        comb3 = sb("comb3", [P, NPAIR, CW], BF16)
        combT = sb("combT", [CW, TG], BF16)
        CB = sb("CB", [P, NC - 1, TG])
        HB = [sb(f"HB{n}", [P, TG]) for n in range(3)]
        st = [sb(f"st{k}", [P, NPAIR, 6]) for k in range(3)]
        mv = [sb(f"mv{k}", [P, NPAIR, 2]) for k in range(3)]
        ve = [sb(f"ve{k}", [P, NPAIR]) for k in range(3)]
        rs = [sb(f"rs{k}", [P, NPAIR]) for k in range(3)]

        s_ident = sem("s_ident"); s_bqk = sem("s_bqk"); s_wv = sem("s_wv")
        s_wqk = [sem("s_wqk0"), sem("s_wqk1")]; s_w = sem("s_w"); s_w13 = sem("s_w13"); s_wrest = sem("s_wrest")
        s_xin = sem("s_xin"); s_xres = sem("s_xres"); s_ctx = sem("s_ctx"); s_out = sem("s_out")
        act_w = sem("act_w"); dve_w = sem("dve_w"); pool_w = sem("pool_w")
        pe_bias = sem("pe_bias"); dve_bias = sem("dve_bias")
        act_w13 = sem("act_w13"); dve_w13 = sem("dve_w13")
        ln_st = [sem(f"ln_st{k}") for k in range(3)]
        ln_mv = [sem(f"ln_mv{k}") for k in range(3)]
        ln_ve = [sem(f"ln_ve{k}") for k in range(3)]
        ln_rs = [sem(f"ln_rs{k}") for k in range(3)]
        ln_xh = [sem(f"ln_xh{k}") for k in range(3)]
        pe_axT = sem("pe_axT"); act_axT = sem("act_axT"); dve_axlo = sem("dve_axlo")
        pe_qkv = sem("pe_qkv"); act_k = sem("act_k"); act_q = sem("act_q"); dve_k = sem("dve_k")
        act_v = sem("act_v"); pool_xres = sem("pool_xres")
        pe_as = sem("pe_as"); dve_amx = sem("dve_amx"); dve_asub = sem("dve_asub"); act_ae = sem("act_ae")
        dve_asm = sem("dve_asm"); dve_ar = sem("dve_ar")
        pe_at = sem("pe_at"); act_apt = sem("act_apt"); pe_apv = sem("pe_apv"); dve_az = sem("dve_az")
        pe_azt = sem("pe_azt"); act_azt = sem("act_azt"); pe_apr = sem("pe_apr"); dve_x1 = sem("dve_x1")
        pool_x1b = sem("pool_x1b")
        pe_bxT = sem("pe_bxT"); act_bxT = sem("act_bxT"); pe_bqk = sem("pe_bqk"); act_bqk = sem("act_bqk")
        pe_bv = sem("pe_bv"); act_bv = sem("act_bv"); pool_kbd = sem("pool_kbd")
        pe_bs = sem("pe_bs"); dve_bmx = sem("dve_bmx"); dve_bsub = sem("dve_bsub"); act_be = sem("act_be")
        dve_br = sem("dve_br")
        pe_bt = sem("pe_bt"); act_bpt = sem("act_bpt"); pe_bpv = sem("pe_bpv"); dve_bz = sem("dve_bz")
        pe_bzt = sem("pe_bzt"); act_bzt = sem("act_bzt"); pe_bo = sem("pe_bo"); dve_x2 = sem("dve_x2")
        dve_x2b = sem("dve_x2b")
        pe_cxT = sem("pe_cxT"); act_cxT = sem("act_cxT"); dve_cxlo = sem("dve_cxlo")
        pe_lg = sem("pe_lg"); dve_route_chain = sem("dve_route_chain"); dve_part = sem("dve_part"); act_tl = sem("act_tl"); dve_route = sem("dve_route"); dve_comb = sem("dve_comb")
        pe_ct = sem("pe_ct"); act_ct = sem("act_ct"); pe_cb = sem("pe_cb"); act_cb = sem("act_cb")
        pe_gu = sem("pe_gu"); act_gu = sem("act_gu"); dve_p1 = sem("dve_p1"); dve_p2 = sem("dve_p2")
        pool_h = sem("pool_h"); pe_dn = sem("pe_dn"); dve_out = sem("dve_out")

        s_zw = sem("s_zw"); s_zr = sem("s_zr")
        N_W, N_WREST = 9, 3

        CB_MASK, CB_LOWER = (NC - 1) * P, (NC - 1) * P + HU * SEQ

        z_dram = nc.dram_tensor("z_dram", [NPAIR, H, P, DC], F32, kind="Internal").ap()
        x_g = x.rearrange("(g t p) e -> g p t e", t=NPAIR, p=P)
        ctx_g = ctx_in.rearrange("(g t p) e -> g p t e", t=NPAIR, p=P)
        xr_g = x_hba.rearrange("(g t p) e -> g p t e", t=NPAIR, p=P)
        out_g = out.rearrange("(g t p) e -> g p t e", t=NPAIR, p=P)

        def due(count):
            return not isinstance(count, int) or count > 0

        def run(eng, walk):
            def once(i):
                for step, n, behind in schedule():
                    if not isinstance(i, int) or 0 <= i - behind < GROUPS:
                        walk(step, n, i - behind)

            for i in range(LAG + 1):
                once(i)
            with eng.Fori(LAG + 1, GROUPS) as i:
                once(i)
            for i in range(GROUPS, GROUPS + LAG):
                once(i)

        block = stack.enter_context(nc.Block())

        @block.sync
        def _(sp):
            for dst, src, done in (
                    (ident[:], c_ident, s_ident), (xin[:], x_g[0], s_xin),
                    (w13_in[:].rearrange("p a n -> p (a n)")[:, 0:2 * JU * P], w_qk[:, 0:2 * JU * P], s_wqk[0]),
                    (bqk[:].rearrange("p a j -> p (a j)"), b_qk, s_bqk),
                    (w13_in[:].rearrange("p a n -> p (a n)")[:, 2 * JU * P:2 * NJ * P],
                     w_qk[:, 2 * JU * P:2 * NJ * P], s_wqk[1]),
                    (wv[:].rearrange("p a n -> p (a n)"), w_v, s_wv),
                    (CB[:].rearrange("p c t -> p (c t)")[:, CB_MASK:CB_MASK + HU * SEQ], c_mask, s_w),
                    (CB[:].rearrange("p c t -> p (c t)")[:, CB_LOWER:CB_LOWER + NE * NE], c_lower, s_w),
                    (wproj[:].rearrange("p j e -> p (j e)"), w_proj, s_w), (bv_t[:], b_v, s_w),
                    (wc[:].rearrange("p a e -> p (a e)"), wc_qkvo, s_w), (bcqk[:], bc_qk, s_w),
                    (bcv_t[:], bc_v, s_w), (bo[:], bc_o, s_w), (head[:], c_head, s_w)):
                sp.dma_start(dst, src).then_inc(done, 16)
            sp.wait_ge(dve_w, 2)
            sp.dma_start(w13_in[:].rearrange("p a n -> p (a n)"), w13).then_inc(s_w13, 16)
            sp.dma_start(CB[:].rearrange("p c t -> p (c t)")[0:CW, 0:CB_MASK], c_sel).then_inc(s_w13, 16)
            for dst, src in ((gw[:], gate_w), (gb[:], gate_b), (w2s[:].rearrange("p c e -> p (c e)"), w2)):
                sp.dma_start(dst, src).then_inc(s_wrest, 16)

            def a_ln(n, g):
                if due(g):
                    sp.wait_ge(ln_xh[0], g)
                    sp.dma_start(xin[:], x_g[g]).then_inc(s_xin, 16)

            def b_ln(n, g):
                if due(g):
                    sp.wait_ge(pe_bxT, g)
                sp.dma_start(cin[:], ctx_g[g]).then_inc(s_ctx, 16)

            def a_s(u, g):
                if u == 0:
                    if due(NPAIR * g):
                        sp.wait_ge(dve_x1, NPAIR * g)
                    sp.dma_start(xres[:], xr_g[g]).then_inc(s_xres, 16)

            does = {"a_ln": a_ln, "a_s": a_s, "b_ln": b_ln}

            def walk(step, n, g):
                if step in does:
                    does[step](n, g)

            run(sp, walk)

        @block.tensor
        def _(pe):
            mm, tr = nc.tensor.matmul, nc.tensor.transpose

            def split_product(o, w_hi, w_lo, x_hi, x_lo):
                mm(o, w_hi, x_hi, start=True, stop=False)
                mm(o, w_lo, x_hi, start=False, stop=False)
                return mm(o, w_hi, x_lo, start=False, stop=True)

            def a_xT(n, g):
                pe.wait_ge(ln_xh[0], g + 1)
                if due(NPAIR * g):
                    pe.wait_ge(dve_x1, NPAIR * g)
                for t in range(NPAIR):
                    last = tr(XA[:, t * P:(t + 1) * P], xh1[:, t, :], ident[:])
                last.then_inc(pe_axT, 1)

            def a_qk(j, g):
                if j == 0:
                    pe.wait_ge(act_axT, 2 * (g + 1))
                    pe.wait_ge(dve_axlo, g + 1)
                    if due(NU * g):
                        pe.wait_ge(dve_asub, NU * g)
                if j >= 3:
                    pe.wait_ge(act_q, NJ * g + j - 2)
                b = RING[j % 3]
                jh, jj = j // JU, j % JU
                split_product(b[:, 0:TG], wqk_hi[:, jh, 0, jj, :], wqk_lo[:, jh, 0, jj, :],
                              xT_hi[:], xT_lo[:])
                split_product(b[:, TG:2 * TG], wqk_hi[:, jh, 1, jj, :], wqk_lo[:, jh, 1, jj, :],
                              xT_hi[:], xT_lo[:]).then_inc(pe_qkv, 1)

            def a_v(b, g):
                n = NJ + b
                if n - 3 < NJ:
                    pe.wait_ge(act_q, NJ * g + n - 2)
                else:
                    pe.wait_ge(act_v, NB * g + n - 2 - NJ)
                for h2 in range(2):
                    last = mm(RING[n % 3][64 * h2:64 * h2 + 64, :], xT[:, b * SEQ:(b + 1) * SEQ],
                              wv[:, h2, :], start=True, stop=True)
                last.then_inc(pe_qkv, 1)

            def a_s(u, g):
                p, hf = u // 2, u % 2
                if u == 0:
                    pe.wait_ge(act_k, NJ * (g + 1))
                    pe.wait_ge(act_q, NJ * (g + 1))
                    pe.wait_ge(dve_k, NJ * (g + 1))
                if u < 2:
                    pe.wait_ge(act_v, NB * g + u + 2)
                else:
                    if due(NU * g + u - 1):
                        pe.wait_ge(dve_asub, NU * g + u - 1)
                S = SA[u % 2]
                mm(S[:], identb[:], maskb[:].rearrange("p h k -> p (h k)"), start=True, stop=False,
                   skip_group_check=True)
                for jj in range(JU):
                    for b2 in range(2):
                        b = 2 * p + b2
                        last = mm(S[64 * b2:64 * b2 + 64, jj * P:(jj + 1) * P],
                                  QT[:, JU * hf + jj, b * SEQ:(b + 1) * SEQ],
                                  KT[:, JU * hf + jj, b, :, :].rearrange("p h k -> p (h k)"),
                                  start=False, stop=True, skip_group_check=True)
                last.then_inc(pe_as, 1)

            def a_t(u, g):
                pe.wait_ge(act_ae, NU * g + u + 1)
                if u == 0:
                    pe.wait_ge(act_v, NB * (g + 1))
                elif u % 2:
                    if due(NU * g + u):
                        pe.wait_ge(act_azt, NU * g + u)
                else:
                    if due(NPAIR * g + u // 2):
                        pe.wait_ge(dve_x1, NPAIR * g + u // 2)
                for jj in range(JU):
                    last = tr(XA[:, jj * P:(jj + 1) * P], DA[u % 2][:, jj * P:(jj + 1) * P], ident[:])
                last.then_inc(pe_at, 1)

            def a_pv(u, g):
                p, hf = u // 2, u % 2
                pe.wait_ge(act_apt, NU * g + u + 1)
                for jj in range(JU):
                    for b2 in range(2):
                        last = mm(XA[64 * b2:64 * b2 + 64, jj * P:(jj + 1) * P],
                                  PTA[:, jj * P + 64 * b2:jj * P + 64 * b2 + 64],
                                  V[:, 2 * p + b2, JU * hf + jj, :, :].rearrange("p h d -> p (h d)"),
                                  start=True, stop=True)
                last.then_inc(pe_apv, 1)

            def a_zt(u, g):
                pe.wait_ge(dve_az, NU * g + u + 1)
                for jj in range(JU):
                    last = tr(XA[:, jj * P:(jj + 1) * P], zA[:, jj * P:(jj + 1) * P], ident[:])
                last.then_inc(pe_azt, 1)

            def a_pr(p, g):
                pe.wait_ge(act_azt, NU * g + 2 * p + 2)
                for r in range(NR2):
                    last = mm(XA[:, 0:E], zT[:, r, p, :, :].rearrange("p h c -> p (h c)"),
                              wproj[:, r, :], start=(r == 0), stop=(r == NR2 - 1))
                last.then_inc(pe_apr, 1)

            def b_xT(n, g):
                pe.wait_ge(ln_xh[1], g + 1)
                pe.wait_ge(s_ctx, 16 * (g + 1))
                if due(NPAIR * g):
                    pe.wait_ge(dve_x2, NPAIR * g)
                for t in range(NPAIR):
                    tr(XB[:, t * P:(t + 1) * P], xh2[:, t, :], ident[:])
                for t in range(NPAIR):
                    last = tr(XB[:, TG + t * P:TG + (t + 1) * P], cin[:, t, :], ident[:])
                last.then_inc(pe_bxT, 1)

            def b_qk(n, g):
                pe.wait_ge(act_bxT, g + 1)
                if due(NU * g):
                    pe.wait_ge(dve_bsub, NU * g)
                for a in range(2):
                    last = mm(SB[:, a * TG:(a + 1) * TG], wc[:, a, :], xcT[:, a, :], start=True, stop=True)
                last.then_inc(pe_bqk, 1)

            def b_v(n, g):
                pe.wait_ge(act_bxT, g + 1)
                for b in range(NB):
                    for h2 in range(2):
                        last = mm(XB[64 * h2:64 * h2 + 64, b * E:(b + 1) * E],
                                  xcT[:, 1, b * SEQ:(b + 1) * SEQ], wc[:, 2, :], start=True, stop=True)
                last.then_inc(pe_bv, 1)

            def b_s(u, g):
                p, hf = u // 2, u % 2
                pe.wait_ge(pool_kbd, NB * g + 2 * p + 2)
                if u == 0:
                    pe.wait_ge(act_bqk, 2 * (g + 1))
                else:
                    if due(NU * g + u):
                        pe.wait_ge(dve_bsub, NU * g + u)
                for b2 in range(2):
                    b = 2 * p + b2
                    last = mm(SB[64 * b2:64 * b2 + 64, :], QcT[:, b * SEQ:(b + 1) * SEQ],
                              KBD[:, p, b2, HU * hf:HU * (hf + 1), :].rearrange("p h k -> p (h k)"),
                              start=True, stop=True)
                last.then_inc(pe_bs, 1)

            def b_t(u, g):
                pe.wait_ge(act_be, NU * g + u + 1)
                if u == 0:
                    pe.wait_ge(act_bv, 2 * (g + 1))
                elif u < 3:
                    if due(NU * g + u):
                        pe.wait_ge(dve_bz, NU * g + u)
                else:
                    pe.wait_ge(dve_x2, NPAIR * g + 1)
                for jj in range(JU):
                    last = tr(XB[:, jj * P:(jj + 1) * P], DB[u % 2][:, jj * P:(jj + 1) * P], ident[:])
                last.then_inc(pe_bt, 1)

            def b_pv(u, g):
                p, hf = u // 2, u % 2
                pe.wait_ge(act_bpt, NU * g + u + 1)
                for jj in range(JU):
                    for b2 in range(2):
                        first = (E + 4 - CW) * hf
                        last = mm(XB[64 * b2:64 * b2 + 64, jj * CW:(jj + 1) * CW],
                                  PTB[:, jj * P + 64 * b2:jj * P + 64 * b2 + 64],
                                  Vc[:, 2 * p + b2, first:first + CW], start=True, stop=True)
                last.then_inc(pe_bpv, 1)

            def b_zt(p, g):
                if due(16 * (NPAIR * g + p + 1)):
                    pe.wait_ge(s_zr, 16 * (NPAIR * g + p + 1))
                pe.wait_ge(dve_bz, NU * g + 3 + p)
                tr(XB[:, 0:P], zr[:, p, :], ident[:]).then_inc(pe_bzt, 1)

            def b_o(p, g):
                pe.wait_ge(act_bzt, NPAIR * g + p + 1)
                mm(XB[:, 0:E], zcT[:], wc[:, 3, :], start=True, stop=True).then_inc(pe_bo, 1)

            def c_xT(n, g):
                pe.wait_ge(ln_xh[2], g + 1)
                if due(g):
                    pe.wait_ge(dve_out, g)
                for t in range(NPAIR):
                    last = tr(Y[:, t * P:(t + 1) * P], xh3[:, t, :], ident[:])
                last.then_inc(pe_cxT, 1)

            def c_lg(n, g):
                pe.wait_ge(act_cxT, 2 * (g + 1))
                if due(NC * g):
                    pe.wait_ge(dve_p2, NC * g)
                for t in range(NPAIR):
                    last = mm(GU[0][:, t * NE:(t + 1) * NE], x3T[:, t * P:(t + 1) * P], gw[:],
                              start=True, stop=True)
                last.then_inc(pe_lg, 1)

            def c_ct(n, g):
                pe.wait_ge(dve_comb, g + 1)
                o = GU[1][:].bitcast(BF16)
                for t in range(NPAIR):
                    last = tr(o[0:CW, t * P:(t + 1) * P], comb3[:, t, :], identb[:])
                last.then_inc(pe_ct, 1)

            def c_cb(k, g):
                if k == 0:
                    pe.wait_ge(act_ct, g + 1)
                    pe.wait_ge(act_tl, g + 1)
                elif k >= 2:
                    pe.wait_ge(act_cb, NCB * g + k - 1)
                for a in range(2):
                    last = mm(GU[k % 2][:, a * TG:(a + 1) * TG], selb[:, 2 * k + a, :], combT[:],
                              start=True, stop=True)
                last.then_inc(pe_cb, 1)

            def c_gu(c, g):
                if c == 0:
                    pe.wait_ge(dve_cxlo, g + 1)
                if c < 2:
                    pe.wait_ge(act_cb, NCB * g + NCB - 1 + c)
                else:
                    pe.wait_ge(dve_p2, NC * g + c - 1)
                m = P if c < NC - 1 else NI
                cols = slice(c * P, c * P + m)
                for a in range(2):
                    last = split_product(GU[c % 2][0:m, a * TG:(a + 1) * TG], w13_hi[:, a, cols],
                                         w13_lo[:, a, cols], x3_hi[:], x3_lo[:])
                last.then_inc(pe_gu, 1)

            def c_dn(c, g):
                m = P if c < NC - 1 else NI
                if c < NC - 1:
                    pe.wait_ge(pool_h, (NC - 1) * g + c + 1)
                else:
                    pe.wait_ge(dve_p2, NC * (g + 1))
                for t in range(NPAIR):
                    last = mm(Y[:, t * E:(t + 1) * E], HB[c % 3][0:m, t * P:(t + 1) * P],
                              w2s[0:m, c, :], start=(c == 0 and t == 0), stop=(c == NC - 1),
                              skip_group_check=True)
                last.then_inc(pe_dn, 1)

            does = {"a_xT": a_xT, "a_qk": a_qk, "a_v": a_v, "a_s": a_s, "a_t": a_t, "a_pv": a_pv,
                    "a_zt": a_zt, "a_pr": a_pr, "b_xT": b_xT, "b_qk": b_qk, "b_v": b_v, "b_s": b_s,
                    "b_t": b_t, "b_pv": b_pv, "b_zt": b_zt, "b_o": b_o, "c_xT": c_xT, "c_lg": c_lg,
                    "c_ct": c_ct, "c_cb": c_cb, "c_gu": c_gu, "c_dn": c_dn}

            def walk(step, n, g):
                if isinstance(g, int) and g == 0 and (step, n) in first_time:
                    first_time[step, n]()
                if step in does:
                    does[step](n, g)

            def weights_qk():
                pe.wait_ge(act_w, 2)
                pe.wait_ge(dve_w, 1)

            def weights_qk_rest():
                pe.wait_ge(act_w, 3)
                pe.wait_ge(dve_w, 2)

            def weights_v():
                pe.wait_ge(s_wv, 16)

            def weights():
                pe.wait_ge(s_w, 16 * N_W)
                pe.wait_ge(act_w, 5)
                pe.wait_ge(pool_w, 9)
                for r in range(NR2):
                    mm(SB[:, 0:E], bv_t[:], wproj[:, r, :], start=(r == 0), stop=(r == NR2 - 1))
                mm(XB[:, 0:E], bcv_t[:], wc[:, 3, :], start=True, stop=True).then_inc(pe_bias, 1)

            def weights_b():
                pe.wait_ge(dve_bias, 2)

            def weights_13():
                pe.wait_ge(act_w13, 2)
                pe.wait_ge(dve_w13, 1)
                pe.wait_ge(s_wrest, 16 * N_WREST)

            first_time = {("a_qk", 0): weights_qk, ("a_qk", JU): weights_qk_rest, ("a_v", 0): weights_v, ("a_s", 0): weights,
                          ("b_xT", 0): weights_b, ("c_ln", 0): weights_13}

            pe.wait_ge(s_ident, 16)
            pe.wait_ge(act_w, 1)
            run(pe, walk)

        @block.scalar
        def _(act):
            func, copy = nc.scalar.activation, nc.scalar.copy

            def a_xT(n, g):
                act.wait_ge(pe_axT, g + 1)
                copy(xT[:], XA[:, 0:TG]).then_inc(act_axT, 1)
                copy(xT_hi[:], XA[:, 0:TG]).then_inc(act_axT, 1)

            def a_qk(j, g):
                b = RING[j % 3]
                act.wait_ge(pe_qkv, NQKV * g + j + 1)
                func(KT[0:64, j, :, 0, :], b[0:64, TG:2 * TG].rearrange("p (b k) -> p b k", k=SEQ),
                     ACT.Identity, bias=bqk[0:64, 1, j:j + 1]).then_inc(act_k, 1)
                act.wait_ge(dve_k, NJ * g + j + 1)
                func(QT[:, j, :], b[:, 0:TG], ACT.Identity, bias=bqk[:, 0, j:j + 1]).then_inc(act_q, 1)

            def a_v(b, g):
                act.wait_ge(pe_qkv, NQKV * g + NJ + b + 1)
                for h2 in range(2):
                    half_p = slice(64 * h2, 64 * h2 + 64)
                    last = copy(V[half_p, b, :, h2, :],
                                RING[(NJ + b) % 3][half_p, :].rearrange("p (j d) -> p j d", d=DH))
                last.then_inc(act_v, 1)

            def a_s(u, g):
                act.wait_ge(dve_asub, NU * g + u + 1)
                func(DA[u % 2][:], DA[u % 2][:], ACT.Exp, scale=DH ** -0.5).then_inc(act_ae, 1)

            def a_t(u, g):
                act.wait_ge(pe_at, NU * g + u + 1)
                copy(PTA[:], XA[:]).then_inc(act_apt, 1)

            def a_zt(u, g):
                p, hf = u // 2, u % 2
                act.wait_ge(pe_azt, NU * g + u + 1)
                for h2 in range(2):
                    src = XA[64 * h2:64 * h2 + 64, :].rearrange("p (j c r s) -> p s r j c", j=JU, c=2 * NA, s=2)
                    for r2 in range(2):
                        last = copy(zT[64 * r2:64 * r2 + 64, :, p, HU * hf + h2:HU * (hf + 1):2, :],
                                    src[:, r2, :, :, :])
                last.then_inc(act_azt, 1)

            def b_xT(n, g):
                act.wait_ge(pe_bxT, g + 1)
                for t in range(NPAIR):
                    copy(xcT[:, 0, t * P:(t + 1) * P].rearrange("p (b h a) -> p b h a", b=2, h=H),
                         XB[:, t * P:(t + 1) * P].rearrange("p (h b a) -> p b h a", b=2, h=H))
                copy(xcT[:, 1, :], XB[:, TG:2 * TG]).then_inc(act_bxT, 1)

            def b_qk(n, g):
                act.wait_ge(pe_bqk, g + 1)
                if due(NB * g):
                    act.wait_ge(pool_kbd, NB * g)
                for a, dst in enumerate((QcT, KcT)):
                    func(dst[:], SB[:, a * TG:(a + 1) * TG], ACT.Identity,
                         bias=bcqk[:, a:a + 1]).then_inc(act_bqk, 1)

            def b_v(n, g):
                act.wait_ge(pe_bv, g + 1)
                for h2 in range(2):
                    half_p = slice(64 * h2, 64 * h2 + 64)
                    copy(Vc[half_p, :, 2:2 + E]
                         .rearrange("p b (j h d) -> p b j h d", j=NJ, h=2)[:, :, :, h2, :],
                         XB[half_p, :].rearrange("p (b j h d) -> p b j h d", b=NB, j=NJ, h=2)[:, :, :, h2, :])\
                        .then_inc(act_bv, 1)

            def b_s(u, g):
                act.wait_ge(dve_bsub, NU * g + u + 1)
                func(DB[u % 2][:], DB[u % 2][:], ACT.Exp, scale=DC ** -0.5).then_inc(act_be, 1)

            def b_t(u, g):
                act.wait_ge(pe_bt, NU * g + u + 1)
                copy(PTB[:], XB[:]).then_inc(act_bpt, 1)

            def b_write(p, g):
                act.wait_ge(dve_bz, NU * g + 2 * p + 2)
                if due(NPAIR * (g - 1) + p + 1):
                    act.wait_ge(pe_bzt, NPAIR * (g - 1) + p + 1)
                act.dma_start(z_dram[p].rearrange("h q d -> q h d"),
                              zc[:, p, :].rearrange("q (h d) -> q h d", d=DC)).then_inc(s_zw, 16)

            def b_back(p, g):
                if due(16 * (NPAIR * g + p + 1)):
                    act.wait_ge(s_zw, 16 * (NPAIR * g + p + 1))
                act.dma_start(zr[:, p, :], z_dram[p].rearrange("h (c r) d -> (h c) (r d)", r=NR))\
                    .then_inc(s_zr, 16)

            def b_zt(p, g):
                act.wait_ge(pe_bzt, NPAIR * g + p + 1)
                copy(zcT[:], XB[:, 0:P]).then_inc(act_bzt, 1)

            def c_xT(n, g):
                act.wait_ge(pe_cxT, g + 1)
                copy(x3T[:], Y[:, 0:TG]).then_inc(act_cxT, 1)
                copy(x3_hi[:], Y[:, 0:TG]).then_inc(act_cxT, 1)

            def c_lg(n, g):
                act.wait_ge(pe_lg, g + 1)
                if due(g):
                    act.wait_ge(dve_route, g)
                func(tl[:].rearrange("p t e -> p (t e)"), GU[0][:, 0:NPAIR * NE], ACT.Tanh,
                     scale=0.5).then_inc(act_tl, 1)

            def c_ct(n, g):
                act.wait_ge(pe_ct, g + 1)
                copy(combT[:], GU[1][:].bitcast(BF16)[0:CW, 0:TG]).then_inc(act_ct, 1)

            def c_cb(k, g):
                act.wait_ge(pe_cb, NCB * g + k + 1)
                if due((NC - 1) * (g - 1) + 2 * k + 2):
                    act.wait_ge(pool_h, (NC - 1) * (g - 1) + 2 * k + 2)
                copy(CB[:, 2 * k:2 * k + 2, :].rearrange("p c t -> p (c t)"),
                     GU[k % 2][:]).then_inc(act_cb, 1)

            def c_gu(c, g):
                m = P if c < NC - 1 else NI
                act.wait_ge(pe_gu, NC * g + c + 1)
                if due(NC * g + c - 2):
                    act.wait_ge(pe_dn, NC * g + c - 2)
                func(HB[c % 3][0:m, :], GU[c % 2][0:m, 0:TG], ACT.Tanh, scale=0.5).then_inc(act_gu, 1)

            def c_out(n, g):
                act.wait_ge(dve_out, g + 1)
                act.dma_start(out_g[g], yo[:]).then_inc(s_out, 16)

            does = {"a_xT": a_xT, "a_qk": a_qk, "a_v": a_v, "a_s": a_s, "a_t": a_t, "a_zt": a_zt,
                    "b_xT": b_xT, "b_qk": b_qk, "b_v": b_v, "b_s": b_s, "b_t": b_t, "b_zt": b_zt,
                    "b_write": b_write, "b_back": b_back, "c_xT": c_xT, "c_lg": c_lg, "c_ct": c_ct,
                    "c_cb": c_cb, "c_gu": c_gu, "c_out": c_out}

            def walk(step, n, g):
                if step == "a_v" and n == 0 and isinstance(g, int) and g == 0:
                    act.wait_ge(pool_w, 3)
                if step == "a_s" and n == 0 and isinstance(g, int) and g == 0:
                    constants()
                if step == "b_ln" and isinstance(g, int) and g == 0:
                    weights_13()
                if step in does:
                    does[step](n, g)

            def weights_13():
                act.wait_ge(s_w13, 32)
                copy(w13_hi[:], w13_in[:]).then_inc(act_w13, 1)
                copy(selb[:].rearrange("p c m -> p (c m)"),
                     CB[:].rearrange("p c t -> p (c t)")[0:CW, 0:(NC - 1) * P]).then_inc(act_w13, 1)

            def constants():
                act.wait_ge(s_w, 16 * N_W)
                copy(maskb[:].rearrange("p h k -> p (h k)"),
                     CB[:].rearrange("p c t -> p (c t)")[:, CB_MASK:CB_MASK + HU * SEQ]).then_inc(act_w, 1)
                copy(lowerb[:].rearrange("p e f -> p (e f)"),
                     CB[:].rearrange("p c t -> p (c t)")[:, CB_LOWER:CB_LOWER + NE * NE]).then_inc(act_w, 1)
                act.wait_ge(pool_w, 9)

            act.wait_ge(s_ident, 16)
            copy(identb[:], ident[:]).then_inc(act_w, 1)
            for jh in range(2):
                act.wait_ge(s_wqk[jh], 16)
                copy(wqk_hi[:, jh].rearrange("p a j n -> p (a j n)"),
                     w13_in[:].rearrange("p a n -> p (a n)")[:, 2 * JU * P * jh:2 * JU * P * (jh + 1)])\
                    .then_inc(act_w, 1)
            act.wait_ge(s_bqk, 16)
            act.wait_ge(pool_w, 2)
            run(act, walk)
            act.wait_ge(s_out, 16 * GROUPS)

        @block.vector
        def _(dve):
            tt, ts, stt, red = (nc.vector.tensor_tensor, nc.vector.tensor_scalar,
                                nc.vector.scalar_tensor_tensor, nc.vector.tensor_reduce)

            def ln(k, src, g):
                for t in range(NPAIR):
                    last = nc.vector.bn_stats(st[k][:, t, :], src[:, t, :])
                last.then_inc(ln_st[k], 1)
                dve.wait_ge(ln_st[k], g + 1)
                nc.vector.memset(gate[:], 0.0)
                for t in range(NPAIR):
                    last = nc.vector.bn_aggr(mv[k][:, t, :], st[k][:, t, :])
                last.then_inc(ln_mv[k], 1)
                dve.wait_ge(ln_mv[k], g + 1)
                ts(ve[k][:], mv[k][:, :, 1], EPS, None, ALU.add).then_inc(ln_ve[k], 1)

            def norm(k, src, dst, g):
                dve.wait_ge(ln_rs[k], g + 1)
                for t in range(NPAIR):
                    last = ts(dst[:, t, :], src[:, t, :], mv[k][:, t, 0:1], rs[k][:, t:t + 1],
                              ALU.subtract, ALU.mult)
                last.then_inc(ln_xh[k], 1)

            def a_ln(n, g):
                dve.wait_ge(s_xin, 16 * (g + 1))
                ln(0, xin, g)

            def a_norm(n, g):
                if due(g):
                    dve.wait_ge(pe_axT, g)
                norm(0, xin, xh1, g)

            def a_xT(n, g):
                dve.wait_ge(act_axT, 2 * (g + 1))
                tt(xT_lo[:], XA[:, 0:TG], xT_hi[:].bitcast(F32), ALU.subtract).then_inc(dve_axlo, 1)

            def a_qk(j, g):
                dve.wait_ge(pe_qkv, NQKV * g + j + 1)
                ts(KT[64:128, j, :, 1, :],
                   RING[j % 3][64:128, TG:2 * TG].rearrange("p (b k) -> p b k", k=SEQ),
                   bqk[64:128, 1, j:j + 1], None, ALU.add).then_inc(dve_k, 1)

            def softmax_shift(u, g, S, D, mx, pe_s, s_mx, s_sub, pe_t):
                dve.wait_ge(pe_s, NU * g + u + 1)
                if due(NU * g + u):
                    dve.wait_ge(s_sub, NU * g + u)
                red(mx[:], S[:].rearrange("p (h k) -> p h k", k=SEQ), AX_X, ALU.max).then_inc(s_mx, 1)
                dve.wait_ge(s_mx, NU * g + u + 1)
                if due(NU * g + u - 1):
                    dve.wait_ge(pe_t, NU * g + u - 1)
                tt(D[u % 2][:].rearrange("p (h k) -> p h k", k=SEQ),
                   S[:].rearrange("p (h k) -> p h k", k=SEQ),
                   mx[:].unsqueeze(2).to_broadcast([P, HU, SEQ]), ALU.subtract).then_inc(s_sub, 1)

            def a_s(u, g):
                softmax_shift(u, g, SA[u % 2], DA, mxA, pe_as, dve_amx, dve_asub, pe_at)

            def a_t(u, g):
                dve.wait_ge(act_ae, NU * g + u + 1)
                if due(NU * g + u):
                    dve.wait_ge(dve_ar, NU * g + u)
                red(smA[:], DA[u % 2][:].rearrange("p (h k) -> p h k", k=SEQ), AX_X, ALU.add)\
                    .then_inc(dve_asm, 1)
                dve.wait_ge(dve_asm, NU * g + u + 1)
                nc.vector.reciprocal(rA[:, u % 2, :], smA[:]).then_inc(dve_ar, 1)

            def a_pv(u, g):
                dve.wait_ge(pe_apv, NU * g + u + 1)
                dve.wait_ge(dve_ar, NU * g + u + 1)
                if due(NU * g + u):
                    dve.wait_ge(pe_azt, NU * g + u)
                tt(zA[:].rearrange("p (h d) -> p h d", d=DH), XA[:].rearrange("p (h d) -> p h d", d=DH),
                   rA[:, u % 2, :].unsqueeze(2).to_broadcast([P, HU, DH]), ALU.mult).then_inc(dve_az, 1)

            def a_pr(p, g):
                dve.wait_ge(pe_apr, NPAIR * g + p + 1)
                if p == 0:
                    dve.wait_ge(pool_xres, g + 1)
                    if due(g):
                        dve.wait_ge(pool_x1b, g)
                    if due(g):
                        dve.wait_ge(ln_xh[1], g)
                stt(X1[:, p, :], XA[:, 0:E], DH ** -0.5, xres[:, p, :], ALU.mult, ALU.add)\
                    .then_inc(dve_x1, 1)

            def b_ln(n, g):
                dve.wait_ge(dve_x1, NPAIR * (g + 1))
                ln(1, X1, g)

            def b_norm(n, g):
                if due(g):
                    dve.wait_ge(pe_bxT, g)
                norm(1, X1, xh2, g)

            def b_s(u, g):
                softmax_shift(u, g, SB, DB, mxB, pe_bs, dve_bmx, dve_bsub, pe_bt)

            def b_pv(u, g):
                p, hf = u // 2, u % 2
                dve.wait_ge(pe_bpv, NU * g + u + 1)
                if due(NU * g + u):
                    dve.wait_ge(dve_bz, NU * g + u)
                ones = (CW - 2) * hf
                nc.vector.reciprocal(
                    rB[:], XB[:, 0:JU * CW].rearrange("p (j c) -> p j c", j=JU)[:, :, ones:ones + 2])\
                    .then_inc(dve_br, 1)
                dve.wait_ge(dve_br, NU * g + u + 1)
                if due(16 * (NPAIR * (g - 1) + p + 1)):
                    dve.wait_ge(s_zw, 16 * (NPAIR * (g - 1) + p + 1))
                own = 2 - 2 * hf + (E // 2 - E - 2 + CW) * hf
                own = XB[:, own:own + JU * (CW + 2 * DC)]
                own = own.rearrange("p (j c) -> p j c", j=JU)[:, :, 0:2 * DC]
                tt(zc[:, p, 64 * hf:64 * hf + 64].rearrange("p (j h d) -> p j h d", j=JU, h=2),
                   own.rearrange("p j (h d) -> p j h d", h=2),
                   rB[:].unsqueeze(3)
                   .to_broadcast([P, JU, 2, DC]), ALU.mult).then_inc(dve_bz, 1)

            def b_o(p, g):
                dve.wait_ge(pe_bo, NPAIR * g + p + 1)
                if p == 0:
                    dve.wait_ge(pool_x1b, g + 1)
                    if due(g):
                        dve.wait_ge(dve_x2b, g)
                    if due(g):
                        dve.wait_ge(ln_xh[2], g)
                tt(X2[:, p, :], XB[:, 0:E], X1b[:, p, :], ALU.add).then_inc(dve_x2, 1)

            def c_ln(n, g):
                dve.wait_ge(dve_x2, NPAIR * (g + 1))
                ln(2, X2, g)
                if due(g):
                    dve.wait_ge(dve_out, g)
                nc.vector.tensor_copy(X2b[:], X2[:]).then_inc(dve_x2b, 1)

            def c_norm(n, g):
                if due(g):
                    dve.wait_ge(pe_cxT, g)
                norm(2, X2, xh3, g)

            def c_xT(n, g):
                dve.wait_ge(act_cxT, 2 * (g + 1))
                tt(x3_lo[:], Y[:, 0:TG], x3_hi[:].bitcast(F32), ALU.subtract).then_inc(dve_cxlo, 1)

            def c_route(part, g):
                first = [0, 6, 11, 16][part]
                done = [first]

                def link(ins):
                    done[0] += 1
                    ins.then_inc(dve_route_chain, 1)
                    dve.wait_ge(dve_route_chain, CH_R * g + done[0])

                if part == 0:
                    dve.wait_ge(act_tl, g + 1)
                    link(ts(scr[:], tl[:], 0.5, 0.5, ALU.mult, ALU.add))
                    link(tt(sbias[:], scr[:], gb[:].unsqueeze(1).to_broadcast([P, NPAIR, NE]), ALU.add))
                    pairs = sbias[:].rearrange("p t (g a b) -> p (t g) a b", a=2, b=2)
                    tt(pmx[:], pairs[:, :, :, 0], pairs[:, :, :, 1], ALU.max)
                    link(tt(pmn[:], pairs[:, :, :, 0], pairs[:, :, :, 1], ALU.min))
                    gs_f = gs[:].rearrange("p t g -> p (t g)")
                    tt(pmn[:], pmx[:], pmn[:], ALU.add)
                    link(tt(gs_f, pmx[:, :, 0], pmx[:, :, 1], ALU.add))
                    link(tt(gs_f, gs_f, pmn[:, :, 0], ALU.max))
                    link(tt(gs_f, gs_f, pmn[:, :, 1], ALU.max))
                elif part == 1:
                    other = gs[:].unsqueeze(2).to_broadcast([P, NPAIR, NG, NG])
                    own = gs[:].unsqueeze(3).to_broadcast([P, NPAIR, NG, NG])
                    lower = lowerb[:, 0:NG, 0:NG].unsqueeze(1).to_broadcast([P, NPAIR, NG, NG])
                    tt(g_gt[:], other, own, ALU.is_gt)
                    link(tt(g_eq[:], other, own, ALU.is_equal))
                    link(tt(g_eq[:], g_eq[:], lower, ALU.mult))
                    link(tt(g_gt[:], g_gt[:], g_eq[:], ALU.add))
                    link(red(gcnt[:], g_gt[:], AX_X, ALU.add))
                    link(ts(gcnt[:], gcnt[:], 1.5, NEG, ALU.is_gt, ALU.mult))
                elif part == 2:
                    by_group = gcnt[:].rearrange("p t g -> p (t g)").unsqueeze(2)
                    flat = sbias[:].rearrange("p t (g e) -> p (t g) e", e=EG)
                    link(tt(flat, flat, by_group.to_broadcast([P, NPAIR * NG, EG]), ALU.add))
                    other = sbias[:].unsqueeze(2).to_broadcast([P, NPAIR, NE, NE])
                    own = sbias[:].unsqueeze(3).to_broadcast([P, NPAIR, NE, NE])
                    lower = lowerb[:].unsqueeze(1).to_broadcast([P, NPAIR, NE, NE])
                    tt(e_gt[:], other, own, ALU.is_gt)
                    link(tt(e_eq[:], other, own, ALU.is_equal))
                    link(tt(e_eq[:], e_eq[:], lower, ALU.mult))
                    link(tt(e_gt[:], e_gt[:], e_eq[:], ALU.add))
                    link(red(ecnt[:], e_gt[:], AX_X, ALU.add))
                else:
                    if due(g):
                        dve.wait_ge(pe_ct, g)
                    link(stt(wsel[:], ecnt[:], 3.5, scr[:], ALU.is_lt, ALU.mult))
                    link(red(wsum[:], wsel[:], AX_X, ALU.add))
                    link(ts(wsum[:], wsum[:], 1e-20, None, ALU.add))
                    link(nc.vector.reciprocal(wsum[:], wsum[:]))
                    link(stt(wsel[:], wsel[:], 2.5, wsum[:].unsqueeze(2).to_broadcast([P, NPAIR, NE]),
                             ALU.mult, ALU.mult))
                    nc.vector.tensor_copy(comb3[:, :, 0:NE], wsel[:]).then_inc(dve_route, 1)
                    dve.wait_ge(dve_route, g + 1)
                    tt(wsel[:], wsel[:], comb3[:, :, 0:NE], ALU.subtract).then_inc(dve_part, 1)
                    dve.wait_ge(dve_part, 3 * g + 1)
                    nc.vector.tensor_copy(comb3[:, :, 32:32 + NE], wsel[:]).then_inc(dve_part, 1)
                    dve.wait_ge(dve_part, 3 * g + 2)
                    tt(wsel[:], wsel[:], comb3[:, :, 32:32 + NE], ALU.subtract).then_inc(dve_part, 1)
                    dve.wait_ge(dve_part, 3 * g + 3)
                    nc.vector.tensor_copy(comb3[:, :, 64:64 + NE], wsel[:]).then_inc(dve_comb, 1)

            def c_gu(c, g):
                m = P if c < NC - 1 else NI
                hb = HB[c % 3][0:m, :]
                dve.wait_ge(act_gu, NC * g + c + 1)
                stt(hb, hb, 1.0, GU[c % 2][0:m, 0:TG], ALU.add, ALU.mult).then_inc(dve_p1, 1)
                dve.wait_ge(dve_p1, NC * g + c + 1)
                stt(hb, GU[c % 2][0:m, TG:2 * TG], 0.5, hb, ALU.mult, ALU.mult).then_inc(dve_p2, 1)

            def c_out(n, g):
                dve.wait_ge(pe_dn, NC * (g + 1))
                dve.wait_ge(dve_x2b, g + 1)
                if due(16 * g):
                    dve.wait_ge(s_out, 16 * g)
                tt(yo[:].rearrange("p t e -> p (t e)"), Y[:, 0:TG],
                   X2b[:].rearrange("p t e -> p (t e)"), ALU.add).then_inc(dve_out, 1)

            does = {"a_ln": a_ln, "a_norm": a_norm, "a_xT": a_xT, "a_qk": a_qk, "a_s": a_s,
                    "a_t": a_t, "a_pv": a_pv, "a_pr": a_pr, "b_ln": b_ln, "b_norm": b_norm,
                    "b_s": b_s, "b_pv": b_pv, "b_o": b_o, "c_ln": c_ln, "c_norm": c_norm,
                    "c_xT": c_xT, "c_route": c_route, "c_gu": c_gu, "c_out": c_out}

            def walk(step, n, g):
                if isinstance(g, int) and g == 0 and (step, n) in first_time:
                    first_time[step, n]()
                if step in does:
                    does[step](n, g)

            def weights_qk():
                for jh in range(2):
                    dve.wait_ge(act_w, jh + 2)
                    tt(wqk_lo[:, jh].rearrange("p a j n -> p (a j n)"),
                       w13_in[:].rearrange("p a n -> p (a n)")[:, 2 * JU * P * jh:2 * JU * P * (jh + 1)],
                       wqk_hi[:, jh].rearrange("p a j n -> p (a j n)").bitcast(F32), ALU.subtract)\
                        .then_inc(dve_w, 1)
                dve.wait_ge(s_bqk, 16)
                dve.wait_ge(pool_w, 2)

            def biases():
                dve.wait_ge(s_w, 16 * N_W)
                dve.wait_ge(act_w, 5)
                dve.wait_ge(pool_w, 9)
                dve.wait_ge(pe_bias, 1)
                ts(bias_a[:], SB[:, 0:E], DH ** -0.5, None, ALU.mult).then_inc(dve_bias, 1)
                tt(bias_b[:], XB[:, 0:E], bo[:], ALU.add).then_inc(dve_bias, 1)

            def weights_13():
                dve.wait_ge(act_w13, 1)
                tt(w13_lo[:], w13_in[:], w13_hi[:].bitcast(F32), ALU.subtract).then_inc(dve_w13, 1)
                dve.wait_ge(s_wrest, 16 * N_WREST)

            first_time = {("a_qk", 0): weights_qk, ("a_s", 0): biases, ("b_ln", 0): weights_13}

            run(dve, walk)

        @block.gpsimd
        def _(pool):
            def power(k, g):
                pool.wait_ge(ln_ve[k], g + 1)
                if due(g):
                    pool.wait_ge(ln_xh[k], g)
                nc.gpsimd.tensor_tensor(rs[k][:], ve[k][:], half[:], ALU.pow).then_inc(ln_rs[k], 1)

            def b_kbd(p, g):
                pool.wait_ge(act_bqk, 2 * (g + 1))
                if due(NU * (g - 1) + 2 * p + 2):
                    pool.wait_ge(pe_bs, NU * (g - 1) + 2 * p + 2)
                for b2 in range(2):
                    b = 2 * p + b2
                    nc.gpsimd.tensor_tensor(
                        KBD[:, p, b2, :, :],
                        KcT[:, b * SEQ:(b + 1) * SEQ].unsqueeze(1).to_broadcast([P, H, SEQ]),
                        head[:].unsqueeze(2).to_broadcast([P, H, SEQ]), ALU.mult).then_inc(pool_kbd, 1)

            def c_gu(c, g):
                if c < NC - 1:
                    pool.wait_ge(dve_p2, NC * g + c + 1)
                    pool.wait_ge(act_cb, NCB * g + c // 2 + 1)
                    nc.gpsimd.tensor_tensor(HB[c % 3][:], HB[c % 3][:], CB[:, c, :], ALU.mult)\
                        .then_inc(pool_h, 1)

            def a_s(u, g):
                if u == 0:
                    pool.wait_ge(s_xres, 16 * (g + 1))
                    nc.gpsimd.tensor_tensor(xres[:], xres[:], bias_a[:].unsqueeze(1)
                                            .to_broadcast([P, NPAIR, E]), ALU.add).then_inc(pool_xres, 1)

            def b_xT(n, g):
                pool.wait_ge(dve_x1, NPAIR * (g + 1))
                if due(NPAIR * g):
                    pool.wait_ge(dve_x2, NPAIR * g)
                nc.gpsimd.tensor_tensor(X1b[:], X1[:], bias_b[:].unsqueeze(1)
                                        .to_broadcast([P, NPAIR, E]), ALU.add).then_inc(pool_x1b, 1)

            does = {"a_s": a_s, "b_xT": b_xT,
                    "a_ln": lambda n, g: power(0, g), "b_ln": lambda n, g: power(1, g),
                    "c_ln": lambda n, g: power(2, g), "b_kbd": b_kbd, "c_gu": c_gu}

            def walk(step, n, g):
                if step == "a_s" and n == 0 and isinstance(g, int) and g == 0:
                    pool.wait_ge(s_w, 16 * N_W)
                    pool.wait_ge(dve_bias, 2)
                if step in does:
                    does[step](n, g)

            nc.gpsimd.memset(half[:], -0.5).then_inc(pool_w, 1)
            nc.gpsimd.memset(KT[:], 0.0).then_inc(pool_w, 1)
            nc.gpsimd.memset(V[:], 0.0).then_inc(pool_w, 1)
            nc.gpsimd.memset(Vc[:], 0.0).then_inc(pool_w, 1)
            nc.gpsimd.memset(comb3[:], 0.0).then_inc(pool_w, 1)
            pool.wait_ge(pool_w, 5)
            for h2 in range(2):
                rows = slice(64 * h2, 64 * h2 + 64)
                nc.gpsimd.memset(Vc[rows, :, h2:h2 + 1], 1.0).then_inc(pool_w, 1)
                nc.gpsimd.memset(Vc[rows, :, E + 2 + h2:E + 3 + h2], 1.0).then_inc(pool_w, 1)
            pool.wait_ge(pool_w, 9)
            run(pool, walk)


def kernel(**inputs):
    import numpy as np
    import concourse.bacc as bacc
    from concourse import mybir as mb
    from concourse.bass_utils import run_bass_kernel_spmd

    a = {k: np.asarray(v) for k, v in inputs.items()}

    def heads_t(w):
        return w.reshape(H * DH, E).T

    def by_parity(w):
        return w.reshape(NJ, 2, DH, -1).transpose(3, 1, 0, 2)

    def columns(b):
        return b.reshape(NJ, P).T

    def rows(b, n=P):
        return np.tile(b.reshape(1, -1), (n, 1))

    def by_token(b, n):
        return np.tile(np.repeat(b.reshape(H, n).T, 2 * NA, 1), (P // n, 1))

    w_qk = np.stack([heads_t(a["L0_attn_Wq"]), heads_t(a["L0_attn_Wk"])], 1)
    w1 = np.concatenate([a["L0_ffn_w1"].reshape(FR, E), a["L0_ffn_ws1"]], 0).T
    w3 = np.concatenate([a["L0_ffn_w3"].reshape(FR, E), a["L0_ffn_ws3"]], 0).T
    w2 = np.zeros((NC * P, E), np.float32)
    w2[0:FR] = a["L0_ffn_w2"].transpose(0, 2, 1).reshape(FR, E)
    w2[FR:FR + NI] = a["L0_ffn_ws2"].T
    q = np.arange(P) % SEQ
    mask = np.where(np.arange(SEQ)[None, :] > q[:, None], np.float32(NEG), np.float32(0))
    sel = np.zeros((CW, (NC - 1) * P), np.float32)
    for part in range(3):
        sel[32 * part + np.arange(FR) // NI, np.arange(FR)] = 1
    given = [
        ("x", a["x"].reshape(TOKENS, E)),
        ("x_hba", a["x"].reshape(TOKENS // P, 2, H, NA, E).transpose(0, 2, 1, 3, 4).reshape(TOKENS, E)),
        ("ctx", a["ctx_1024"].reshape(TOKENS, E)),
        ("w_qk", w_qk.reshape(E, 2, 2, JU * P).transpose(0, 2, 1, 3).reshape(E, 2 * NJ * P)),
        ("w_v", by_parity(a["L0_attn_Wv"]).reshape(E, 2 * NJ * DH)),
        ("w_proj", a["L0_attn_proj"].reshape(NJ, P, E).transpose(1, 0, 2).reshape(P, NJ * E)),
        ("b_qk", np.concatenate([columns(a["L0_attn_bq"]), columns(a["L0_attn_bk"])], 1)),
        ("b_v", by_token(a["L0_attn_bv"], DH)),
        ("wc_qkvo", np.concatenate([a["L0_xattn_" + n].T for n in ("Wq", "Wk", "Wv", "Wo")], 1)),
        ("bc_qk", np.stack([a["L0_xattn_bq"], a["L0_xattn_bk"]], 1)),
        ("bc_v", by_token(a["L0_xattn_bv"], DC)), ("bc_o", rows(a["L0_xattn_bo"])),
        ("gate_w", a["L0_ffn_gate_w"].T), ("gate_b", rows(a["L0_ffn_gate_bias"])),
        ("w13", np.concatenate([w1, w3], 1)),
        ("w2", w2.reshape(NC, P, E).transpose(1, 0, 2).reshape(P, NC * E)),
        ("c_ident", np.eye(P, dtype=np.float32)), ("c_mask", np.tile(mask, (1, HU))),
        ("c_head", (np.arange(P)[:, None] // DC == np.arange(H)[None, :]).astype(np.float32)),
        ("c_sel", sel),
        ("c_lower", rows((np.arange(NE)[None, :] < np.arange(NE)[:, None]).astype(np.float32))),
    ]
    nc = bacc.Bacc("TRN2", target_bir_lowering=False, num_devices=1)
    arrays, args = {}, []
    for name, v in given:
        arrays["in_" + name] = np.ascontiguousarray(v)
        args.append(nc.dram_tensor("in_" + name, v.shape, mb.dt.from_np(v.dtype), kind="ExternalInput").ap())
    args.append(nc.dram_tensor("out_0", (TOKENS, E), mb.dt.float32, kind="ExternalOutput").ap())
    decoder_layer(nc, *args)
    r = run_bass_kernel_spmd(nc, [arrays], core_ids=[0])
    o = r.results[0]["out_0"].reshape(TOKENS // P, H, 2, NA, E).transpose(0, 2, 1, 3, 4)
    return np.ascontiguousarray(o).reshape(TOKENS // SEQ, SEQ, E)
```

```python
from contextlib import ExitStack

import concourse.bass as bass
from concourse import mybir

F32 = mybir.dt.float32
F32R = mybir.dt.float32r
BF16 = mybir.dt.bfloat16
ALU = mybir.AluOpType
ACT = mybir.ActivationFunctionType
AX_X = mybir.AxisListType.X

P = 128
E = 128
SEQ = 64
TOKENS = 64 * SEQ
NPAIR = 2
NB = 2 * NPAIR
TG = NPAIR * P
GROUPS = TOKENS // TG
H = 16
DH = 64
NJ = H // 2
DC = E // H
NU = 2 * NPAIR
JU = NJ // 2
HU = H // 2
NE, NI = 16, 96
FR = NE * NI
NC = FR // P + 1
NCB = (NC - 1) // 2
NQKV = NJ + NB
NR, NA = H, SEQ // H
NR2 = NR // 2
NG, EG = 4, NE // 4
EPS = 1e-5
NEG = -1e30
CW = 96

CH_R = 21


ORDERS = {
    "sync": """
        b_ln.0-1 a_ln.0 a_s.0""",
    "tensor": """
        b_t.1-2 a_zt.2-1 b_pv.1-2 a_t.3-1 a_xT.0 a_pv.3-1 a_qk.0 a_qk.1 b_s.3-2 a_zt.3-1 b_t.2-2 a_qk.2
        a_qk.3 a_pr.1-1 b_pv.2-2 a_qk.4 c_ct.0-3 a_qk.5 b_zt.0-2 c_cb.0-3 c_cb.1-3 b_o.0-2 a_qk.6 c_cb.2-3
        b_t.3-2 a_qk.7 c_cb.3-3 c_cb.4-3 b_pv.3-2 a_v.0 c_cb.5-3 c_gu.0-3 a_v.1 a_v.2 c_gu.1-3 a_v.3
        c_gu.2-3 c_dn.0-3 a_s.0 c_gu.3-3 c_dn.1-3 a_s.1 c_gu.4-3 c_dn.2-3 c_gu.5-3 b_zt.1-2 c_dn.3-3 a_t.0
        c_gu.6-3 b_o.1-2 c_dn.4-3 c_gu.7-3 c_dn.5-3 b_xT.0-1 c_gu.8-3 c_dn.6-3 a_pv.0 c_gu.9-3 b_qk.0-1
        c_dn.7-3 c_gu.10-3 a_zt.0 c_dn.8-3 a_s.2 a_t.1 c_gu.11-3 c_dn.9-3 c_gu.12-3 b_v.0-1 a_pv.1 b_s.0-1
        c_dn.10-3 a_zt.1 c_dn.11-3 c_dn.12-3 b_s.1-1 a_pr.0 a_s.3 b_t.0-1 c_xT.0-2 a_t.2 b_pv.0-1 c_lg.0-2
        b_s.2-1 a_pv.2""",
    "scalar": """
        a_zt.2-1 a_t.3-1 a_xT.0 b_write.0-2 a_qk.0 a_qk.1 a_zt.3-1 b_back.0-2 b_s.3-2 b_t.2-2 a_qk.2
        a_qk.3 c_ct.0-3 a_qk.4 b_zt.0-2 c_cb.0-3 a_qk.5 c_cb.1-3 c_cb.2-3 b_t.3-2 a_qk.6 c_cb.3-3 c_cb.4-3
        a_qk.7 a_v.0 c_cb.5-3 c_gu.0-3 a_v.1 b_write.1-2 a_v.2 c_gu.1-3 c_gu.2-3 a_v.3 b_back.1-2 c_gu.3-3
        a_s.0 c_gu.4-3 c_gu.5-3 b_zt.1-2 a_s.1 a_t.0 c_gu.6-3 c_gu.7-3 b_xT.0-1 c_gu.8-3 c_gu.9-3 b_qk.0-1
        c_gu.10-3 a_zt.0 a_s.2 a_t.1 c_gu.11-3 c_gu.12-3 b_v.0-1 a_zt.1 b_s.0-1 b_s.1-1 c_out.0-3 b_t.0-1
        c_xT.0-2 c_lg.0-2 a_s.3 a_t.2 b_s.2-1 b_t.1-1""",
    "vector": """
        a_ln.0 c_route.2-3 c_route.3-3 a_norm.0 c_route.4-3 a_t.3-1 a_xT.0 c_route.5-3 b_pv.1-2 a_pv.3-1
        a_qk.0 a_qk.1 c_route.6-3 b_s.3-2 c_route.7-3 a_qk.2 c_route.8-3 a_qk.3 c_route.9-3 b_pv.2-2
        a_qk.4 a_qk.5 b_o.0-2 a_pr.1-1 a_qk.6 a_qk.7 b_ln.0-1 b_pv.3-2 c_gu.0-3 c_gu.1-3 c_gu.2-3
        b_norm.0-1 a_s.0 c_gu.3-3 a_s.1 c_gu.4-3 c_gu.5-3 c_gu.6-3 b_o.1-2 c_gu.7-3 c_gu.8-3 a_t.0 a_pv.0
        c_gu.9-3 c_gu.10-3 a_s.2 a_t.1 c_gu.11-3 c_gu.12-3 a_pv.1 b_s.0-1 c_out.0-3 c_ln.0-2 b_s.1-1
        c_norm.0-2 a_pr.0 a_s.3 a_t.2 b_pv.0-1 c_xT.0-2 c_route.0-2 b_s.2-1 c_route.1-2 a_pv.2""",
    "gpsimd": """
        a_ln.0 a_s.0 b_ln.0-1 c_gu.0-3 c_gu.1-3 c_gu.2-3 c_gu.3-3 c_gu.4-3 c_gu.5-3 c_gu.6-3 c_gu.7-3
        b_xT.0-1 c_gu.8-3 c_gu.9-3 b_kbd.0-1 c_gu.10-3 c_gu.11-3 c_ln.0-2 b_kbd.1-1""",
}
LAG = 3


def schedule(engine):
    out = []
    for word in ORDERS[engine].split():
        name, _, behind = word.partition("-")
        step, number = name.split(".")
        out.append((step, int(number), int(behind or 0)))
    return out


def decoder_layer(nc, x, x_hba, ctx_in, w_qk, w_v, w_proj, b_qk, b_v, wc_qkvo, bc_qk, bc_v, bc_o,
                  gate_w, gate_b, w13, w2, c_ident, c_mask, c_head, c_sel, c_lower, out):
    with ExitStack() as stack:
        def sb(name, shape, dt=F32):
            return stack.enter_context(nc.sbuf_tensor(name, shape, dt))

        def sem(name):
            return stack.enter_context(nc.semaphore(name))

        def bank(name):
            return stack.enter_context(nc.psum_tensor(name, [P, 512], F32))

        SA = [bank("SA0"), bank("SA1")]
        XA = bank("XA")
        SB, XB = bank("SB"), bank("XB")
        GU = [bank("GU0"), bank("GU1")]
        Y = bank("Y")

        wqk_hi, wqk_lo = (sb(n, [P, 2, 2, JU, P], F32R) for n in ("wqk_hi", "wqk_lo"))
        wv = sb("wv", [P, 2, NJ * DH])
        wproj = sb("wproj", [P, NJ, E])
        bqk = sb("bqk", [P, 2, NJ])
        bv_t, bcv_t = sb("bv_t", [P, P]), sb("bcv_t", [P, P])
        bias_a, bias_b = sb("bias_a", [P, E]), sb("bias_b", [P, E])
        wc = sb("wc", [P, 4, E])
        bcqk, bo = sb("bcqk", [P, 2]), sb("bo", [P, E])
        gw, gb = sb("gw", [P, NE]), sb("gb", [P, NE])
        w13_hi, w13_lo = sb("w13_hi", [P, 2, FR + NI], F32R), sb("w13_lo", [P, 2, FR + NI], F32R)
        w13_in = sb("w13_in", [P, 2, FR + NI])
        w2s = sb("w2s", [P, NC, E])
        ident, identb = sb("ident", [P, P]), sb("identb", [P, P], BF16)
        maskb = sb("maskb", [P, HU, SEQ], BF16)
        head = sb("head", [P, H])
        selb = sb("selb", [CW, NC - 1, P], BF16)
        lowerb = sb("lowerb", [P, NE, NE], BF16)
        half, gate = sb("half", [P, NPAIR]), sb("gate", [P, 1])

        xin, xres = sb("xin", [P, NPAIR, E]), sb("xres", [P, NPAIR, E])
        xh1, X1 = sb("xh1", [P, NPAIR, E]), sb("X1", [P, NPAIR, E])
        xT, xT_hi, xT_lo = sb("xT", [P, TG]), sb("xT_hi", [P, TG], F32R), sb("xT_lo", [P, TG], F32R)
        QT = sb("QT", [P, NJ, TG])
        KT = sb("KT", [P, NJ, NB, 2, SEQ])
        V = sb("V", [P, NB, NJ, 2, DH])
        DA = [sb("DA0", [P, 512]), sb("DA1", [P, 512])]
        PTA, zA, zT = sb("PTA", [P, 512]), sb("zA", [P, 512]), sb("zT", [P, NR2, NPAIR, H, 2 * NA])
        mxA, smA, rA = sb("mxA", [P, HU]), sb("smA", [P, HU]), sb("rA", [P, 2, HU])
        cin = sb("cin", [P, NPAIR, E])
        xh2, X1b, X2 = sb("xh2", [P, NPAIR, E]), sb("X1b", [P, NPAIR, E]), sb("X2", [P, NPAIR, E])
        xcT = sb("xcT", [P, 2, TG])
        QcT, KcT = sb("QcT", [P, TG]), sb("KcT", [P, TG])
        KBD = sb("KBD", [P, NPAIR, 2, H, SEQ])
        Vc = sb("Vc", [P, NB, E + 4])
        DB = [sb("DB0", [P, 512]), sb("DB1", [P, 512])]
        PTB, zcT = sb("PTB", [P, 512]), sb("zcT", [P, P])
        zc, zr = sb("zc", [P, NPAIR, E]), sb("zr", [P, NPAIR, E])
        mxB, rB = sb("mxB", [P, HU]), sb("rB", [P, JU, 2])
        xh3, X2b, yo = sb("xh3", [P, NPAIR, E]), sb("X2b", [P, NPAIR, E]), sb("yo", [P, NPAIR, E])
        x3T, x3_hi, x3_lo = sb("x3T", [P, TG]), sb("x3_hi", [P, TG], F32R), sb("x3_lo", [P, TG], F32R)
        tl = sb("tl", [P, NPAIR, NE])
        scr, sbias, wsel = (sb(n, [P, NPAIR, NE]) for n in ("scr", "sbias", "wsel"))
        pmx, pmn = sb("pmx", [P, NPAIR * NG, 2]), sb("pmn", [P, NPAIR * NG, 2])
        gs, gcnt = sb("gs", [P, NPAIR, NG]), sb("gcnt", [P, NPAIR, NG])
        g_gt, g_eq = sb("g_gt", [P, NPAIR, NG, NG], BF16), sb("g_eq", [P, NPAIR, NG, NG], BF16)
        e_gt, e_eq = sb("e_gt", [P, NPAIR, NE, NE], BF16), sb("e_eq", [P, NPAIR, NE, NE], BF16)
        ecnt, wsum = sb("ecnt", [P, NPAIR, NE]), sb("wsum", [P, NPAIR])
        comb3 = sb("comb3", [P, NPAIR, CW], BF16)
        combT = sb("combT", [CW, TG], BF16)
        CB = sb("CB", [P, NC - 1, TG])
        HB = [sb(f"HB{n}", [P, TG]) for n in range(3)]
        st = [sb(f"st{k}", [P, NPAIR, 6]) for k in range(3)]
        mv = [sb(f"mv{k}", [P, NPAIR, 2]) for k in range(3)]
        ve = [sb(f"ve{k}", [P, NPAIR]) for k in range(3)]
        rs = [sb(f"rs{k}", [P, NPAIR]) for k in range(3)]

        s_ident = sem("s_ident"); s_bqk = sem("s_bqk"); s_wv = sem("s_wv")
        s_wqk = [sem("s_wqk0"), sem("s_wqk1")]; s_w = sem("s_w"); s_w13 = sem("s_w13"); s_wrest = sem("s_wrest")
        s_xin = sem("s_xin"); s_xres = sem("s_xres"); s_ctx = sem("s_ctx"); s_out = sem("s_out")
        act_w = sem("act_w"); dve_w = sem("dve_w"); pool_w = sem("pool_w"); dve_zero = sem("dve_zero")
        pe_bias = sem("pe_bias"); dve_bias = sem("dve_bias")
        act_w13 = sem("act_w13"); dve_w13 = sem("dve_w13")
        ln_st = [sem(f"ln_st{k}") for k in range(3)]
        ln_mv = [sem(f"ln_mv{k}") for k in range(3)]
        ln_ve = [sem(f"ln_ve{k}") for k in range(3)]
        ln_rs = [sem(f"ln_rs{k}") for k in range(3)]
        ln_xh = [sem(f"ln_xh{k}") for k in range(3)]
        pe_axT = sem("pe_axT"); act_axhi = sem("act_axhi"); act_axT = sem("act_axT"); dve_axlo = sem("dve_axlo")
        pe_qkv = sem("pe_qkv"); act_k = sem("act_k"); act_q = sem("act_q"); dve_k = sem("dve_k")
        act_v = sem("act_v"); pool_xres = sem("pool_xres")
        pe_as = sem("pe_as"); dve_amx = sem("dve_amx"); dve_asub = sem("dve_asub"); act_ae = sem("act_ae")
        dve_asm = sem("dve_asm"); dve_ar = sem("dve_ar")
        pe_at = sem("pe_at"); act_apt = sem("act_apt"); pe_apv = sem("pe_apv"); dve_az = sem("dve_az")
        pe_azt = sem("pe_azt"); act_azt = sem("act_azt"); pe_apr = sem("pe_apr"); dve_x1 = sem("dve_x1")
        pool_x1b = sem("pool_x1b")
        pe_bxT = sem("pe_bxT"); act_bxT = sem("act_bxT"); pe_bqk = sem("pe_bqk"); act_bqk = sem("act_bqk")
        pe_bv = sem("pe_bv"); act_bv = sem("act_bv"); pool_kbd = sem("pool_kbd")
        pe_bs = sem("pe_bs"); dve_bmx = sem("dve_bmx"); dve_bsub = sem("dve_bsub"); act_be = sem("act_be")
        dve_br = sem("dve_br")
        pe_bt = sem("pe_bt"); act_bpt = sem("act_bpt"); pe_bpv = sem("pe_bpv"); dve_bz = sem("dve_bz")
        pe_bzt = sem("pe_bzt"); act_bzt = sem("act_bzt"); pe_bo = sem("pe_bo"); dve_x2 = sem("dve_x2")
        dve_x2b = sem("dve_x2b")
        pe_cxT = sem("pe_cxT"); act_cxT = sem("act_cxT"); dve_cxlo = sem("dve_cxlo")
        pe_lg = sem("pe_lg"); act_tl = sem("act_tl"); dve_route_chain = sem("dve_route_chain")
        dve_route = sem("dve_route"); dve_part = sem("dve_part"); dve_comb = sem("dve_comb")
        pe_ct = sem("pe_ct"); act_ct = sem("act_ct"); pe_cb = sem("pe_cb"); act_cb = sem("act_cb")
        pe_gu = sem("pe_gu"); act_gu = sem("act_gu"); dve_p1 = sem("dve_p1"); dve_p2 = sem("dve_p2")
        pool_h = sem("pool_h"); pe_dn = sem("pe_dn"); dve_out = sem("dve_out")

        s_zw = sem("s_zw"); s_zr = sem("s_zr")
        N_W, N_WREST = 9, 3

        CB_MASK, CB_LOWER = (NC - 1) * P, (NC - 1) * P + HU * SEQ

        z_dram = nc.dram_tensor("z_dram", [NPAIR, H, P, DC], F32, kind="Internal").ap()
        x_g = x.rearrange("(g t p) e -> g p t e", t=NPAIR, p=P)
        ctx_g = ctx_in.rearrange("(g t p) e -> g p t e", t=NPAIR, p=P)
        xr_g = x_hba.rearrange("(g t p) e -> g p t e", t=NPAIR, p=P)
        out_g = out.rearrange("(g t p) e -> g p t e", t=NPAIR, p=P)

        def due(count):
            return not isinstance(count, int) or count > 0

        def run(eng, engine, walk):
            def once(i):
                for step, n, behind in schedule(engine):
                    if not isinstance(i, int) or 0 <= i - behind < GROUPS:
                        walk(step, n, i - behind)

            for i in range(LAG + 1):
                once(i)
            with eng.Fori(LAG + 1, GROUPS) as i:
                once(i)
            for i in range(GROUPS, GROUPS + LAG):
                once(i)

        block = stack.enter_context(nc.Block())

        @block.sync
        def _(sp):
            for dst, src, done in (
                    (ident[:], c_ident, s_ident), (xin[:], x_g[0], s_xin),
                    (w13_in[:].rearrange("p a n -> p (a n)")[:, 0:2 * JU * P], w_qk[:, 0:2 * JU * P], s_wqk[0]),
                    (bqk[:].rearrange("p a j -> p (a j)"), b_qk, s_bqk),
                    (w13_in[:].rearrange("p a n -> p (a n)")[:, 2 * JU * P:2 * NJ * P],
                     w_qk[:, 2 * JU * P:2 * NJ * P], s_wqk[1]),
                    (wv[:].rearrange("p a n -> p (a n)"), w_v, s_wv),
                    (CB[:].rearrange("p c t -> p (c t)")[:, CB_MASK:CB_MASK + HU * SEQ], c_mask, s_w),
                    (CB[:].rearrange("p c t -> p (c t)")[:, CB_LOWER:CB_LOWER + NE * NE], c_lower, s_w),
                    (wproj[:].rearrange("p j e -> p (j e)"), w_proj, s_w), (bv_t[:], b_v, s_w),
                    (wc[:].rearrange("p a e -> p (a e)"), wc_qkvo, s_w), (bcqk[:], bc_qk, s_w),
                    (bcv_t[:], bc_v, s_w), (bo[:], bc_o, s_w), (head[:], c_head, s_w)):
                sp.dma_start(dst, src).then_inc(done, 16)
            sp.wait_ge(dve_w, 2)
            sp.dma_start(w13_in[:].rearrange("p a n -> p (a n)"), w13).then_inc(s_w13, 16)
            sp.dma_start(CB[:].rearrange("p c t -> p (c t)")[0:CW, 0:CB_MASK], c_sel).then_inc(s_w13, 16)
            for dst, src in ((gw[:], gate_w), (gb[:], gate_b), (w2s[:].rearrange("p c e -> p (c e)"), w2)):
                sp.dma_start(dst, src).then_inc(s_wrest, 16)

            def a_ln(n, g):
                if due(g):
                    sp.wait_ge(ln_xh[0], g)
                    sp.dma_start(xin[:], x_g[g]).then_inc(s_xin, 16)

            def b_ln(n, g):
                if due(g):
                    sp.wait_ge(pe_bxT, g)
                sp.dma_start(cin[:], ctx_g[g]).then_inc(s_ctx, 16)

            def a_s(u, g):
                if u == 0:
                    if due(NPAIR * g):
                        sp.wait_ge(dve_x1, NPAIR * g)
                    sp.dma_start(xres[:], xr_g[g]).then_inc(s_xres, 16)

            does = {"a_ln": a_ln, "a_s": a_s, "b_ln": b_ln}

            def walk(step, n, g):
                if step in does:
                    does[step](n, g)

            run(sp, "sync", walk)

        @block.tensor
        def _(pe):
            mm, tr = nc.tensor.matmul, nc.tensor.transpose

            def split_product(o, w_hi, w_lo, x_hi, x_lo):
                mm(o, w_hi, x_hi, start=True, stop=False)
                mm(o, w_lo, x_hi, start=False, stop=False)
                return mm(o, w_hi, x_lo, start=False, stop=True)

            def a_xT(n, g):
                pe.wait_ge(ln_xh[0], g + 1)
                if due(NU * g):
                    pe.wait_ge(dve_asub, NU * g)
                for t in range(NPAIR):
                    last = tr(SA[1][:, t * P:(t + 1) * P], xh1[:, t, :], ident[:])
                last.then_inc(pe_axT, 1)

            def a_qk(j, g):
                if j == 0:
                    pe.wait_ge(act_axhi, g + 1)
                    pe.wait_ge(dve_axlo, g + 1)
                if j == 1:
                    pe.wait_ge(act_axT, g + 1)
                if j >= 2:
                    pe.wait_ge(act_q, NJ * g + j - 1)
                b = SA[j % 2]
                jh, jj = j // JU, j % JU
                split_product(b[:, 0:TG], wqk_hi[:, jh, 0, jj, :], wqk_lo[:, jh, 0, jj, :],
                              xT_hi[:], xT_lo[:])
                split_product(b[:, TG:2 * TG], wqk_hi[:, jh, 1, jj, :], wqk_lo[:, jh, 1, jj, :],
                              xT_hi[:], xT_lo[:]).then_inc(pe_qkv, 1)

            def a_v(b, g):
                n = NJ + b
                if n - 2 < NJ:
                    pe.wait_ge(act_q, NJ * g + n - 1)
                else:
                    pe.wait_ge(act_v, NB * g + b - 1)
                for h2 in range(2):
                    last = mm(SA[n % 2][64 * h2:64 * h2 + 64, :], xT[:, b * SEQ:(b + 1) * SEQ],
                              wv[:, h2, :], start=True, stop=True)
                last.then_inc(pe_qkv, 1)

            def a_s(u, g):
                p, hf = u // 2, u % 2
                if u == 0:
                    pe.wait_ge(act_k, NJ * (g + 1))
                    pe.wait_ge(act_q, NJ * (g + 1))
                    pe.wait_ge(dve_k, NJ * (g + 1))
                if u < 2:
                    pe.wait_ge(act_v, NB * g + u + 3)
                else:
                    if due(NU * g + u - 1):
                        pe.wait_ge(dve_asub, NU * g + u - 1)
                S = SA[u % 2]
                mm(S[:], identb[:], maskb[:].rearrange("p h k -> p (h k)"), start=True, stop=False,
                   skip_group_check=True)
                for jj in range(JU):
                    for b2 in range(2):
                        b = 2 * p + b2
                        last = mm(S[64 * b2:64 * b2 + 64, jj * P:(jj + 1) * P],
                                  QT[:, JU * hf + jj, b * SEQ:(b + 1) * SEQ],
                                  KT[:, JU * hf + jj, b, :, :].rearrange("p h k -> p (h k)"),
                                  start=False, stop=True, skip_group_check=True)
                last.then_inc(pe_as, 1)

            def a_t(u, g):
                pe.wait_ge(act_ae, NU * g + u + 1)
                if u == 0:
                    pe.wait_ge(act_v, NB * (g + 1))
                    if due(NPAIR * g):
                        pe.wait_ge(dve_x1, NPAIR * g)
                elif u % 2:
                    if due(NU * g + u):
                        pe.wait_ge(act_azt, NU * g + u)
                else:
                    if due(NPAIR * g + u // 2):
                        pe.wait_ge(dve_x1, NPAIR * g + u // 2)
                for jj in range(JU):
                    last = tr(XA[:, jj * P:(jj + 1) * P], DA[u % 2][:, jj * P:(jj + 1) * P], ident[:])
                last.then_inc(pe_at, 1)

            def a_pv(u, g):
                p, hf = u // 2, u % 2
                pe.wait_ge(act_apt, NU * g + u + 1)
                for jj in range(JU):
                    for b2 in range(2):
                        last = mm(XA[64 * b2:64 * b2 + 64, jj * P:(jj + 1) * P],
                                  PTA[:, jj * P + 64 * b2:jj * P + 64 * b2 + 64],
                                  V[:, 2 * p + b2, JU * hf + jj, :, :].rearrange("p h d -> p (h d)"),
                                  start=True, stop=True)
                last.then_inc(pe_apv, 1)

            def a_zt(u, g):
                pe.wait_ge(dve_az, NU * g + u + 1)
                for jj in range(JU):
                    last = tr(XA[:, jj * P:(jj + 1) * P], zA[:, jj * P:(jj + 1) * P], ident[:])
                last.then_inc(pe_azt, 1)

            def a_pr(p, g):
                pe.wait_ge(act_azt, NU * g + 2 * p + 2)
                for r in range(NR2):
                    last = mm(XA[:, 0:E], zT[:, r, p, :, :].rearrange("p h c -> p (h c)"),
                              wproj[:, r, :], start=(r == 0), stop=(r == NR2 - 1))
                last.then_inc(pe_apr, 1)

            def b_xT(n, g):
                pe.wait_ge(ln_xh[1], g + 1)
                pe.wait_ge(s_ctx, 16 * (g + 1))
                if due(NU * g):
                    pe.wait_ge(dve_bsub, NU * g)
                for t in range(NPAIR):
                    tr(SB[:, t * P:(t + 1) * P], xh2[:, t, :], ident[:])
                for t in range(NPAIR):
                    last = tr(SB[:, TG + t * P:TG + (t + 1) * P], cin[:, t, :], ident[:])
                last.then_inc(pe_bxT, 1)

            def b_qk(n, g):
                pe.wait_ge(act_bxT, g + 1)
                for a in range(2):
                    last = mm(SB[:, a * TG:(a + 1) * TG], wc[:, a, :], xcT[:, a, :], start=True, stop=True)
                last.then_inc(pe_bqk, 1)

            def b_v(n, g):
                pe.wait_ge(act_bqk, 2 * (g + 1))
                for b in range(NB):
                    for h2 in range(2):
                        last = mm(SB[64 * h2:64 * h2 + 64, b * E:(b + 1) * E],
                                  xcT[:, 1, b * SEQ:(b + 1) * SEQ], wc[:, 2, :], start=True, stop=True)
                last.then_inc(pe_bv, 1)

            def b_s(u, g):
                p, hf = u // 2, u % 2
                pe.wait_ge(pool_kbd, NB * g + 2 * p + 2)
                if u == 0:
                    pe.wait_ge(act_bv, 2 * (g + 1))
                else:
                    if due(NU * g + u):
                        pe.wait_ge(dve_bsub, NU * g + u)
                for b2 in range(2):
                    b = 2 * p + b2
                    last = mm(SB[64 * b2:64 * b2 + 64, :], QcT[:, b * SEQ:(b + 1) * SEQ],
                              KBD[:, p, b2, HU * hf:HU * (hf + 1), :].rearrange("p h k -> p (h k)"),
                              start=True, stop=True)
                last.then_inc(pe_bs, 1)

            def b_t(u, g):
                pe.wait_ge(act_be, NU * g + u + 1)
                if u == 0:
                    if due(NPAIR * g):
                        pe.wait_ge(dve_x2, NPAIR * g)
                elif u < 3:
                    if due(NU * g + u):
                        pe.wait_ge(dve_bz, NU * g + u)
                else:
                    pe.wait_ge(dve_x2, NPAIR * g + 1)
                for jj in range(JU):
                    last = tr(XB[:, jj * P:(jj + 1) * P], DB[u % 2][:, jj * P:(jj + 1) * P], ident[:])
                last.then_inc(pe_bt, 1)

            def b_pv(u, g):
                p, hf = u // 2, u % 2
                pe.wait_ge(act_bpt, NU * g + u + 1)
                for jj in range(JU):
                    for b2 in range(2):
                        first = (E + 4 - CW) * hf
                        last = mm(XB[64 * b2:64 * b2 + 64, jj * CW:(jj + 1) * CW],
                                  PTB[:, jj * P + 64 * b2:jj * P + 64 * b2 + 64],
                                  Vc[:, 2 * p + b2, first:first + CW], start=True, stop=True)
                last.then_inc(pe_bpv, 1)

            def b_zt(p, g):
                if due(16 * (NPAIR * g + p + 1)):
                    pe.wait_ge(s_zr, 16 * (NPAIR * g + p + 1))
                pe.wait_ge(dve_bz, NU * g + 3 + p)
                tr(XB[:, 0:P], zr[:, p, :], ident[:]).then_inc(pe_bzt, 1)

            def b_o(p, g):
                pe.wait_ge(act_bzt, NPAIR * g + p + 1)
                mm(XB[:, 0:E], zcT[:], wc[:, 3, :], start=True, stop=True).then_inc(pe_bo, 1)

            def c_xT(n, g):
                pe.wait_ge(ln_xh[2], g + 1)
                if due(g):
                    pe.wait_ge(dve_out, g)
                for t in range(NPAIR):
                    last = tr(Y[:, t * P:(t + 1) * P], xh3[:, t, :], ident[:])
                last.then_inc(pe_cxT, 1)

            def c_lg(n, g):
                pe.wait_ge(act_cxT, 2 * g + 1)
                if due(NC * g):
                    pe.wait_ge(dve_p2, NC * g)
                for t in range(NPAIR):
                    last = mm(GU[0][:, t * NE:(t + 1) * NE], x3T[:, t * P:(t + 1) * P], gw[:],
                              start=True, stop=True)
                last.then_inc(pe_lg, 1)

            def c_ct(n, g):
                pe.wait_ge(dve_comb, g + 1)
                o = GU[1][:].bitcast(BF16)
                for t in range(NPAIR):
                    last = tr(o[0:CW, t * P:(t + 1) * P], comb3[:, t, :], identb[:])
                last.then_inc(pe_ct, 1)

            def c_cb(k, g):
                if k == 0:
                    pe.wait_ge(act_ct, g + 1)
                    pe.wait_ge(act_tl, g + 1)
                elif k >= 2:
                    pe.wait_ge(act_cb, NCB * g + k - 1)
                for a in range(2):
                    last = mm(GU[k % 2][:, a * TG:(a + 1) * TG], selb[:, 2 * k + a, :], combT[:],
                              start=True, stop=True)
                last.then_inc(pe_cb, 1)

            def c_gu(c, g):
                if c == 0:
                    pe.wait_ge(dve_cxlo, g + 1)
                if c < 2:
                    pe.wait_ge(act_cb, NCB * g + NCB - 1 + c)
                else:
                    pe.wait_ge(dve_p2, NC * g + c - 1)
                m = P if c < NC - 1 else NI
                cols = slice(c * P, c * P + m)
                for a in range(2):
                    last = split_product(GU[c % 2][0:m, a * TG:(a + 1) * TG], w13_hi[:, a, cols],
                                         w13_lo[:, a, cols], x3_hi[:], x3_lo[:])
                last.then_inc(pe_gu, 1)

            def c_dn(c, g):
                m = P if c < NC - 1 else NI
                if c < NC - 1:
                    pe.wait_ge(pool_h, (NC - 1) * g + c + 1)
                else:
                    pe.wait_ge(dve_p2, NC * (g + 1))
                for t in range(NPAIR):
                    last = mm(Y[:, t * E:(t + 1) * E], HB[c % 3][0:m, t * P:(t + 1) * P],
                              w2s[0:m, c, :], start=(c == 0 and t == 0), stop=(c == NC - 1),
                              skip_group_check=True)
                last.then_inc(pe_dn, 1)

            does = {"a_xT": a_xT, "a_qk": a_qk, "a_v": a_v, "a_s": a_s, "a_t": a_t, "a_pv": a_pv,
                    "a_zt": a_zt, "a_pr": a_pr, "b_xT": b_xT, "b_qk": b_qk, "b_v": b_v, "b_s": b_s,
                    "b_t": b_t, "b_pv": b_pv, "b_zt": b_zt, "b_o": b_o, "c_xT": c_xT, "c_lg": c_lg,
                    "c_ct": c_ct, "c_cb": c_cb, "c_gu": c_gu, "c_dn": c_dn}

            def walk(step, n, g):
                if isinstance(g, int) and g == 0 and (step, n) in first_time:
                    first_time[step, n]()
                if step in does:
                    does[step](n, g)

            def weights_qk():
                pe.wait_ge(act_w, 2)
                pe.wait_ge(dve_w, 1)

            def weights_qk_rest():
                pe.wait_ge(act_w, 3)
                pe.wait_ge(dve_w, 2)

            def weights_v():
                pe.wait_ge(s_wv, 16)

            def weights():
                pe.wait_ge(s_w, 16 * N_W)
                pe.wait_ge(act_w, 5)
                pe.wait_ge(pool_w, 8)
                pe.wait_ge(dve_zero, 1)
                for r in range(NR2):
                    mm(SB[:, 0:E], bv_t[:], wproj[:, r, :], start=(r == 0), stop=(r == NR2 - 1))
                mm(XB[:, 0:E], bcv_t[:], wc[:, 3, :], start=True, stop=True).then_inc(pe_bias, 1)

            def weights_b():
                pe.wait_ge(dve_bias, 2)

            def weights_13():
                pe.wait_ge(act_w13, 2)
                pe.wait_ge(dve_w13, 1)
                pe.wait_ge(s_wrest, 16 * N_WREST)

            first_time = {("a_qk", 0): weights_qk, ("a_qk", JU): weights_qk_rest, ("a_v", 0): weights_v, ("a_s", 0): weights,
                          ("b_xT", 0): weights_b, ("c_xT", 0): weights_13}

            pe.wait_ge(s_ident, 16)
            pe.wait_ge(act_w, 1)
            run(pe, "tensor", walk)

        @block.scalar
        def _(act):
            func, copy = nc.scalar.activation, nc.scalar.copy

            def a_xT(n, g):
                act.wait_ge(pe_axT, g + 1)
                copy(xT_hi[:], SA[1][:, 0:TG]).then_inc(act_axhi, 1)
                act.wait_ge(dve_axlo, g + 1)
                copy(xT[:], SA[1][:, 0:TG]).then_inc(act_axT, 1)

            def a_qk(j, g):
                b = SA[j % 2]
                act.wait_ge(pe_qkv, NQKV * g + j + 1)
                func(KT[0:64, j, :, 0, :], b[0:64, TG:2 * TG].rearrange("p (b k) -> p b k", k=SEQ),
                     ACT.Identity, bias=bqk[0:64, 1, j:j + 1]).then_inc(act_k, 1)
                act.wait_ge(dve_k, NJ * g + j + 1)
                func(QT[:, j, :], b[:, 0:TG], ACT.Identity, bias=bqk[:, 0, j:j + 1]).then_inc(act_q, 1)

            def a_v(b, g):
                act.wait_ge(pe_qkv, NQKV * g + NJ + b + 1)
                if b == 0 and due(NU * g):
                    act.wait_ge(pe_apv, NU * g)
                for h2 in range(2):
                    half_p = slice(64 * h2, 64 * h2 + 64)
                    last = copy(V[half_p, b, :, h2, :],
                                SA[(NJ + b) % 2][half_p, :].rearrange("p (j d) -> p j d", d=DH))
                last.then_inc(act_v, 1)

            def a_s(u, g):
                act.wait_ge(dve_asub, NU * g + u + 1)
                func(DA[u % 2][:], DA[u % 2][:], ACT.Exp, scale=DH ** -0.5).then_inc(act_ae, 1)

            def a_t(u, g):
                act.wait_ge(pe_at, NU * g + u + 1)
                copy(PTA[:], XA[:]).then_inc(act_apt, 1)

            def a_zt(u, g):
                p, hf = u // 2, u % 2
                act.wait_ge(pe_azt, NU * g + u + 1)
                for h2 in range(2):
                    src = XA[64 * h2:64 * h2 + 64, :].rearrange("p (j c r s) -> p s r j c", j=JU, c=2 * NA, s=2)
                    for r2 in range(2):
                        last = copy(zT[64 * r2:64 * r2 + 64, :, p, HU * hf + h2:HU * (hf + 1):2, :],
                                    src[:, r2, :, :, :])
                last.then_inc(act_azt, 1)

            def b_xT(n, g):
                act.wait_ge(pe_bxT, g + 1)
                for t in range(NPAIR):
                    copy(xcT[:, 0, t * P:(t + 1) * P].rearrange("p (b h a) -> p b h a", b=2, h=H),
                         SB[:, t * P:(t + 1) * P].rearrange("p (h b a) -> p b h a", b=2, h=H))
                copy(xcT[:, 1, :], SB[:, TG:2 * TG]).then_inc(act_bxT, 1)

            def b_qk(n, g):
                act.wait_ge(pe_bqk, g + 1)
                if due(NB * g):
                    act.wait_ge(pool_kbd, NB * g)
                for a, dst in ((1, KcT), (0, QcT)):
                    func(dst[:], SB[:, a * TG:(a + 1) * TG], ACT.Identity,
                         bias=bcqk[:, a:a + 1]).then_inc(act_bqk, 1)

            def b_v(n, g):
                act.wait_ge(pe_bv, g + 1)
                if due(NU * g):
                    act.wait_ge(pe_bpv, NU * g)
                for h2 in range(2):
                    half_p = slice(64 * h2, 64 * h2 + 64)
                    copy(Vc[half_p, :, 2:2 + E]
                         .rearrange("p b (j h d) -> p b j h d", j=NJ, h=2)[:, :, :, h2, :],
                         SB[half_p, :].rearrange("p (b j h d) -> p b j h d", b=NB, j=NJ, h=2)[:, :, :, h2, :])\
                        .then_inc(act_bv, 1)

            def b_s(u, g):
                act.wait_ge(dve_bsub, NU * g + u + 1)
                func(DB[u % 2][:], DB[u % 2][:], ACT.Exp, scale=DC ** -0.5).then_inc(act_be, 1)

            def b_t(u, g):
                act.wait_ge(pe_bt, NU * g + u + 1)
                copy(PTB[:], XB[:]).then_inc(act_bpt, 1)

            def b_write(p, g):
                act.wait_ge(dve_bz, NU * g + 2 * p + 2)
                if due(NPAIR * (g - 1) + p + 1):
                    act.wait_ge(pe_bzt, NPAIR * (g - 1) + p + 1)
                act.dma_start(z_dram[p].rearrange("h q d -> q h d"),
                              zc[:, p, :].rearrange("q (h d) -> q h d", d=DC)).then_inc(s_zw, 16)

            def b_back(p, g):
                if due(16 * (NPAIR * g + p + 1)):
                    act.wait_ge(s_zw, 16 * (NPAIR * g + p + 1))
                act.dma_start(zr[:, p, :], z_dram[p].rearrange("h (c r) d -> (h c) (r d)", r=NR))\
                    .then_inc(s_zr, 16)

            def b_zt(p, g):
                act.wait_ge(pe_bzt, NPAIR * g + p + 1)
                copy(zcT[:], XB[:, 0:P]).then_inc(act_bzt, 1)

            def c_xT(n, g):
                act.wait_ge(pe_cxT, g + 1)
                copy(x3T[:], Y[:, 0:TG]).then_inc(act_cxT, 1)
                copy(x3_hi[:], Y[:, 0:TG]).then_inc(act_cxT, 1)

            def c_lg(n, g):
                act.wait_ge(pe_lg, g + 1)
                if due(g):
                    act.wait_ge(dve_route, g)
                func(tl[:].rearrange("p t e -> p (t e)"), GU[0][:, 0:NPAIR * NE], ACT.Tanh,
                     scale=0.5).then_inc(act_tl, 1)

            def c_ct(n, g):
                act.wait_ge(pe_ct, g + 1)
                copy(combT[:], GU[1][:].bitcast(BF16)[0:CW, 0:TG]).then_inc(act_ct, 1)

            def c_cb(k, g):
                act.wait_ge(pe_cb, NCB * g + k + 1)
                if due((NC - 1) * (g - 1) + 2 * k + 2):
                    act.wait_ge(pool_h, (NC - 1) * (g - 1) + 2 * k + 2)
                copy(CB[:, 2 * k:2 * k + 2, :].rearrange("p c t -> p (c t)"),
                     GU[k % 2][:]).then_inc(act_cb, 1)

            def c_gu(c, g):
                m = P if c < NC - 1 else NI
                act.wait_ge(pe_gu, NC * g + c + 1)
                if due(NC * g + c - 2):
                    act.wait_ge(pe_dn, NC * g + c - 2)
                func(HB[c % 3][0:m, :], GU[c % 2][0:m, 0:TG], ACT.Tanh, scale=0.5).then_inc(act_gu, 1)

            def c_out(n, g):
                act.wait_ge(dve_out, g + 1)
                act.dma_start(out_g[g], yo[:]).then_inc(s_out, 16)

            does = {"a_xT": a_xT, "a_qk": a_qk, "a_v": a_v, "a_s": a_s, "a_t": a_t, "a_zt": a_zt,
                    "b_xT": b_xT, "b_qk": b_qk, "b_v": b_v, "b_s": b_s, "b_t": b_t, "b_zt": b_zt,
                    "b_write": b_write, "b_back": b_back, "c_xT": c_xT, "c_lg": c_lg, "c_ct": c_ct,
                    "c_cb": c_cb, "c_gu": c_gu, "c_out": c_out}

            def walk(step, n, g):
                if step == "a_v" and n == 0 and isinstance(g, int) and g == 0:
                    act.wait_ge(pool_w, 8)
                if step == "a_s" and n == 0 and isinstance(g, int) and g == 0:
                    constants()
                if step == "b_xT" and isinstance(g, int) and g == 0:
                    weights_13()
                if step in does:
                    does[step](n, g)

            def weights_13():
                act.wait_ge(s_w13, 32)
                copy(w13_hi[:], w13_in[:]).then_inc(act_w13, 1)
                copy(selb[:].rearrange("p c m -> p (c m)"),
                     CB[:].rearrange("p c t -> p (c t)")[0:CW, 0:(NC - 1) * P]).then_inc(act_w13, 1)

            def constants():
                act.wait_ge(s_w, 16 * N_W)
                copy(maskb[:].rearrange("p h k -> p (h k)"),
                     CB[:].rearrange("p c t -> p (c t)")[:, CB_MASK:CB_MASK + HU * SEQ]).then_inc(act_w, 1)
                copy(lowerb[:].rearrange("p e f -> p (e f)"),
                     CB[:].rearrange("p c t -> p (c t)")[:, CB_LOWER:CB_LOWER + NE * NE]).then_inc(act_w, 1)

            act.wait_ge(s_ident, 16)
            copy(identb[:], ident[:]).then_inc(act_w, 1)
            for jh in range(2):
                act.wait_ge(s_wqk[jh], 16)
                copy(wqk_hi[:, jh].rearrange("p a j n -> p (a j n)"),
                     w13_in[:].rearrange("p a n -> p (a n)")[:, 2 * JU * P * jh:2 * JU * P * (jh + 1)])\
                    .then_inc(act_w, 1)
            act.wait_ge(s_bqk, 16)
            act.wait_ge(dve_zero, 1)
            run(act, "scalar", walk)
            act.wait_ge(s_out, 16 * GROUPS)

        @block.vector
        def _(dve):
            tt, ts, stt, red = (nc.vector.tensor_tensor, nc.vector.tensor_scalar,
                                nc.vector.scalar_tensor_tensor, nc.vector.tensor_reduce)

            def ln(k, src, g):
                for t in range(NPAIR):
                    last = nc.vector.bn_stats(st[k][:, t, :], src[:, t, :])
                last.then_inc(ln_st[k], 1)
                dve.wait_ge(ln_st[k], g + 1)
                nc.vector.memset(gate[:], 0.0)
                for t in range(NPAIR):
                    last = nc.vector.bn_aggr(mv[k][:, t, :], st[k][:, t, :])
                last.then_inc(ln_mv[k], 1)
                dve.wait_ge(ln_mv[k], g + 1)
                ts(ve[k][:], mv[k][:, :, 1], EPS, None, ALU.add).then_inc(ln_ve[k], 1)

            def norm(k, src, dst, g):
                dve.wait_ge(ln_rs[k], g + 1)
                for t in range(NPAIR):
                    last = ts(dst[:, t, :], src[:, t, :], mv[k][:, t, 0:1], rs[k][:, t:t + 1],
                              ALU.subtract, ALU.mult)
                last.then_inc(ln_xh[k], 1)

            def a_ln(n, g):
                dve.wait_ge(s_xin, 16 * (g + 1))
                ln(0, xin, g)

            def a_norm(n, g):
                if due(g):
                    dve.wait_ge(pe_axT, g)
                norm(0, xin, xh1, g)

            def a_xT(n, g):
                dve.wait_ge(act_axhi, g + 1)
                tt(xT_lo[:], SA[1][:, 0:TG], xT_hi[:].bitcast(F32), ALU.subtract).then_inc(dve_axlo, 1)

            def a_qk(j, g):
                dve.wait_ge(pe_qkv, NQKV * g + j + 1)
                ts(KT[64:128, j, :, 1, :],
                   SA[j % 2][64:128, TG:2 * TG].rearrange("p (b k) -> p b k", k=SEQ),
                   bqk[64:128, 1, j:j + 1], None, ALU.add).then_inc(dve_k, 1)

            def softmax_shift(u, g, S, D, mx, pe_s, s_mx, s_sub, pe_t):
                dve.wait_ge(pe_s, NU * g + u + 1)
                if due(NU * g + u):
                    dve.wait_ge(s_sub, NU * g + u)
                red(mx[:], S[:].rearrange("p (h k) -> p h k", k=SEQ), AX_X, ALU.max).then_inc(s_mx, 1)
                dve.wait_ge(s_mx, NU * g + u + 1)
                if due(NU * g + u - 1):
                    dve.wait_ge(pe_t, NU * g + u - 1)
                tt(D[u % 2][:].rearrange("p (h k) -> p h k", k=SEQ),
                   S[:].rearrange("p (h k) -> p h k", k=SEQ),
                   mx[:].unsqueeze(2).to_broadcast([P, HU, SEQ]), ALU.subtract).then_inc(s_sub, 1)

            def a_s(u, g):
                softmax_shift(u, g, SA[u % 2], DA, mxA, pe_as, dve_amx, dve_asub, pe_at)

            def a_t(u, g):
                dve.wait_ge(act_ae, NU * g + u + 1)
                if due(NU * g + u):
                    dve.wait_ge(dve_ar, NU * g + u)
                red(smA[:], DA[u % 2][:].rearrange("p (h k) -> p h k", k=SEQ), AX_X, ALU.add)\
                    .then_inc(dve_asm, 1)
                dve.wait_ge(dve_asm, NU * g + u + 1)
                nc.vector.reciprocal(rA[:, u % 2, :], smA[:]).then_inc(dve_ar, 1)

            def a_pv(u, g):
                dve.wait_ge(pe_apv, NU * g + u + 1)
                dve.wait_ge(dve_ar, NU * g + u + 1)
                if due(NU * g + u):
                    dve.wait_ge(pe_azt, NU * g + u)
                tt(zA[:].rearrange("p (h d) -> p h d", d=DH), XA[:].rearrange("p (h d) -> p h d", d=DH),
                   rA[:, u % 2, :].unsqueeze(2).to_broadcast([P, HU, DH]), ALU.mult).then_inc(dve_az, 1)

            def a_pr(p, g):
                dve.wait_ge(pe_apr, NPAIR * g + p + 1)
                if p == 0:
                    dve.wait_ge(pool_xres, g + 1)
                    if due(g):
                        dve.wait_ge(pool_x1b, g)
                    if due(g):
                        dve.wait_ge(ln_xh[1], g)
                stt(X1[:, p, :], XA[:, 0:E], DH ** -0.5, xres[:, p, :], ALU.mult, ALU.add)\
                    .then_inc(dve_x1, 1)

            def b_ln(n, g):
                dve.wait_ge(dve_x1, NPAIR * (g + 1))
                ln(1, X1, g)

            def b_norm(n, g):
                if due(g):
                    dve.wait_ge(pe_bxT, g)
                norm(1, X1, xh2, g)

            def b_s(u, g):
                softmax_shift(u, g, SB, DB, mxB, pe_bs, dve_bmx, dve_bsub, pe_bt)

            def b_pv(u, g):
                p, hf = u // 2, u % 2
                dve.wait_ge(pe_bpv, NU * g + u + 1)
                if due(NU * g + u):
                    dve.wait_ge(dve_bz, NU * g + u)
                ones = (CW - 2) * hf
                nc.vector.reciprocal(
                    rB[:], XB[:, 0:JU * CW].rearrange("p (j c) -> p j c", j=JU)[:, :, ones:ones + 2])\
                    .then_inc(dve_br, 1)
                dve.wait_ge(dve_br, NU * g + u + 1)
                if due(16 * (NPAIR * (g - 1) + p + 1)):
                    dve.wait_ge(s_zw, 16 * (NPAIR * (g - 1) + p + 1))
                first = (CW - 2 - E // 2) if hf else 2
                own = XB[:, first:first + JU * (CW + 2 * DC)]
                own = own.rearrange("p (j c) -> p j c", j=JU)[:, :, 0:2 * DC]
                tt(zc[:, p, 64 * hf:64 * hf + 64].rearrange("p (j h d) -> p j h d", j=JU, h=2),
                   own.rearrange("p j (h d) -> p j h d", h=2),
                   rB[:].unsqueeze(3)
                   .to_broadcast([P, JU, 2, DC]), ALU.mult).then_inc(dve_bz, 1)

            def b_o(p, g):
                dve.wait_ge(pe_bo, NPAIR * g + p + 1)
                if p == 0:
                    dve.wait_ge(pool_x1b, g + 1)
                    if due(g):
                        dve.wait_ge(dve_x2b, g)
                    if due(g):
                        dve.wait_ge(ln_xh[2], g)
                tt(X2[:, p, :], XB[:, 0:E], X1b[:, p, :], ALU.add).then_inc(dve_x2, 1)

            def c_ln(n, g):
                dve.wait_ge(dve_x2, NPAIR * (g + 1))
                ln(2, X2, g)
                if due(g):
                    dve.wait_ge(dve_out, g)
                nc.vector.tensor_copy(X2b[:], X2[:]).then_inc(dve_x2b, 1)

            def c_norm(n, g):
                if due(g):
                    dve.wait_ge(pe_cxT, g)
                norm(2, X2, xh3, g)

            def c_xT(n, g):
                dve.wait_ge(act_cxT, 2 * (g + 1))
                tt(x3_lo[:], Y[:, 0:TG], x3_hi[:].bitcast(F32), ALU.subtract).then_inc(dve_cxlo, 1)

            def c_route(part, g):
                done = [(0, 2, 4, 6, 9, 11, 13, 16, 19, 21)[part]]
                other = sbias[:].unsqueeze(2).to_broadcast([P, NPAIR, NE, NE])
                own = sbias[:].unsqueeze(3).to_broadcast([P, NPAIR, NE, NE])
                lower = lowerb[:].unsqueeze(1).to_broadcast([P, NPAIR, NE, NE])
                g_other = gs[:].unsqueeze(2).to_broadcast([P, NPAIR, NG, NG])
                g_own = gs[:].unsqueeze(3).to_broadcast([P, NPAIR, NG, NG])
                g_lower = lowerb[:, 0:NG, 0:NG].unsqueeze(1).to_broadcast([P, NPAIR, NG, NG])
                pairs = sbias[:].rearrange("p t (g a b) -> p (t g) a b", a=2, b=2)
                gs_f = gs[:].rearrange("p t g -> p (t g)")

                def link(ins):
                    done[0] += 1
                    ins.then_inc(dve_route_chain, 1)
                    dve.wait_ge(dve_route_chain, CH_R * g + done[0])

                if part > 0:
                    dve.wait_ge(dve_route_chain, CH_R * g + done[0])
                if part == 0:
                    dve.wait_ge(act_tl, g + 1)
                    link(ts(scr[:], tl[:], 0.5, 0.5, ALU.mult, ALU.add))
                    tt(sbias[:], scr[:], gb[:].unsqueeze(1).to_broadcast([P, NPAIR, NE]), ALU.add)\
                        .then_inc(dve_route_chain, 1)
                elif part == 1:
                    tt(pmx[:], pairs[:, :, :, 0], pairs[:, :, :, 1], ALU.max)
                    link(tt(pmn[:], pairs[:, :, :, 0], pairs[:, :, :, 1], ALU.min))
                    tt(pmn[:], pmx[:], pmn[:], ALU.add)
                    tt(gs_f, pmx[:, :, 0], pmx[:, :, 1], ALU.add).then_inc(dve_route_chain, 1)
                elif part == 2:
                    link(tt(gs_f, gs_f, pmn[:, :, 0], ALU.max))
                    tt(gs_f, gs_f, pmn[:, :, 1], ALU.max).then_inc(dve_route_chain, 1)
                elif part == 3:
                    tt(g_gt[:], g_other, g_own, ALU.is_gt)
                    link(tt(g_eq[:], g_other, g_own, ALU.is_equal))
                    link(tt(g_eq[:], g_eq[:], g_lower, ALU.mult))
                    tt(g_gt[:], g_gt[:], g_eq[:], ALU.add).then_inc(dve_route_chain, 1)
                elif part == 4:
                    link(red(gcnt[:], g_gt[:], AX_X, ALU.add))
                    ts(gcnt[:], gcnt[:], 1.5, NEG, ALU.is_gt, ALU.mult).then_inc(dve_route_chain, 1)
                elif part == 5:
                    by_group = gcnt[:].rearrange("p t g -> p (t g)").unsqueeze(2)
                    flat = sbias[:].rearrange("p t (g e) -> p (t g) e", e=EG)
                    link(tt(flat, flat, by_group.to_broadcast([P, NPAIR * NG, EG]), ALU.add))
                    tt(e_gt[:], other, own, ALU.is_gt)
                    tt(e_eq[:], other, own, ALU.is_equal).then_inc(dve_route_chain, 1)
                elif part == 6:
                    link(tt(e_eq[:], e_eq[:], lower, ALU.mult))
                    link(tt(e_gt[:], e_gt[:], e_eq[:], ALU.add))
                    red(ecnt[:], e_gt[:], AX_X, ALU.add).then_inc(dve_route_chain, 1)
                elif part == 7:
                    link(stt(wsel[:], ecnt[:], 3.5, scr[:], ALU.is_lt, ALU.mult))
                    link(red(wsum[:], wsel[:], AX_X, ALU.add))
                    ts(wsum[:], wsum[:], 1e-20, None, ALU.add).then_inc(dve_route_chain, 1)
                elif part == 8:
                    link(nc.vector.reciprocal(wsum[:], wsum[:]))
                    stt(wsel[:], wsel[:], 2.5, wsum[:].unsqueeze(2).to_broadcast([P, NPAIR, NE]),
                        ALU.mult, ALU.mult).then_inc(dve_route_chain, 1)
                else:
                    if due(g):
                        dve.wait_ge(pe_ct, g)
                    nc.vector.tensor_copy(comb3[:, :, 0:NE], wsel[:]).then_inc(dve_route, 1)
                    dve.wait_ge(dve_route, g + 1)
                    tt(wsel[:], wsel[:], comb3[:, :, 0:NE], ALU.subtract).then_inc(dve_part, 1)
                    dve.wait_ge(dve_part, 3 * g + 1)
                    nc.vector.tensor_copy(comb3[:, :, 32:32 + NE], wsel[:]).then_inc(dve_part, 1)
                    dve.wait_ge(dve_part, 3 * g + 2)
                    tt(wsel[:], wsel[:], comb3[:, :, 32:32 + NE], ALU.subtract).then_inc(dve_part, 1)
                    dve.wait_ge(dve_part, 3 * g + 3)
                    nc.vector.tensor_copy(comb3[:, :, 64:64 + NE], wsel[:]).then_inc(dve_comb, 1)

            def c_gu(c, g):
                m = P if c < NC - 1 else NI
                hb = HB[c % 3][0:m, :]
                dve.wait_ge(act_gu, NC * g + c + 1)
                stt(hb, hb, 1.0, GU[c % 2][0:m, 0:TG], ALU.add, ALU.mult).then_inc(dve_p1, 1)
                dve.wait_ge(dve_p1, NC * g + c + 1)
                stt(hb, GU[c % 2][0:m, TG:2 * TG], 0.5, hb, ALU.mult, ALU.mult).then_inc(dve_p2, 1)

            def c_out(n, g):
                dve.wait_ge(pe_dn, NC * (g + 1))
                dve.wait_ge(dve_x2b, g + 1)
                if due(16 * g):
                    dve.wait_ge(s_out, 16 * g)
                tt(yo[:].rearrange("p t e -> p (t e)"), Y[:, 0:TG],
                   X2b[:].rearrange("p t e -> p (t e)"), ALU.add).then_inc(dve_out, 1)

            does = {"a_ln": a_ln, "a_norm": a_norm, "a_xT": a_xT, "a_qk": a_qk, "a_s": a_s,
                    "a_t": a_t, "a_pv": a_pv, "a_pr": a_pr, "b_ln": b_ln, "b_norm": b_norm,
                    "b_s": b_s, "b_pv": b_pv, "b_o": b_o, "c_ln": c_ln, "c_norm": c_norm,
                    "c_xT": c_xT, "c_route": c_route, "c_gu": c_gu, "c_out": c_out}

            def walk(step, n, g):
                if isinstance(g, int) and g == 0 and (step, n) in first_time:
                    first_time[step, n]()
                if step in does:
                    does[step](n, g)

            def weights_qk(jh):
                dve.wait_ge(act_w, jh + 2)
                tt(wqk_lo[:, jh].rearrange("p a j n -> p (a j n)"),
                   w13_in[:].rearrange("p a n -> p (a n)")[:, 2 * JU * P * jh:2 * JU * P * (jh + 1)],
                   wqk_hi[:, jh].rearrange("p a j n -> p (a j n)").bitcast(F32), ALU.subtract)\
                    .then_inc(dve_w, 1)

            def weights_qk_rest():
                weights_qk(1)
                dve.wait_ge(s_bqk, 16)
                dve.wait_ge(dve_zero, 1)

            def biases():
                dve.wait_ge(s_w, 16 * N_W)
                dve.wait_ge(act_w, 5)
                dve.wait_ge(pool_w, 8)
                dve.wait_ge(pe_bias, 1)
                ts(bias_a[:], SB[:, 0:E], DH ** -0.5, None, ALU.mult).then_inc(dve_bias, 1)
                tt(bias_b[:], XB[:, 0:E], bo[:], ALU.add).then_inc(dve_bias, 1)

            def weights_13():
                dve.wait_ge(act_w13, 1)
                tt(w13_lo[:], w13_in[:], w13_hi[:].bitcast(F32), ALU.subtract).then_inc(dve_w13, 1)
                dve.wait_ge(s_wrest, 16 * N_WREST)

            first_time = {("a_xT", 0): lambda: weights_qk(0), ("a_qk", 0): weights_qk_rest,
                          ("a_s", 0): biases, ("c_ln", 0): weights_13}

            nc.vector.memset(KT[:], 0.0).then_inc(dve_zero, 1)
            run(dve, "vector", walk)

        @block.gpsimd
        def _(pool):
            def power(k, g):
                pool.wait_ge(ln_ve[k], g + 1)
                if due(g):
                    pool.wait_ge(ln_xh[k], g)
                nc.gpsimd.tensor_tensor(rs[k][:], ve[k][:], half[:], ALU.pow).then_inc(ln_rs[k], 1)

            def b_kbd(p, g):
                pool.wait_ge(act_bqk, 2 * g + 1)
                if due(NU * (g - 1) + 2 * p + 2):
                    pool.wait_ge(pe_bs, NU * (g - 1) + 2 * p + 2)
                for b2 in range(2):
                    b = 2 * p + b2
                    nc.gpsimd.tensor_tensor(
                        KBD[:, p, b2, :, :],
                        KcT[:, b * SEQ:(b + 1) * SEQ].unsqueeze(1).to_broadcast([P, H, SEQ]),
                        head[:].unsqueeze(2).to_broadcast([P, H, SEQ]), ALU.mult).then_inc(pool_kbd, 1)

            def c_gu(c, g):
                if c < NC - 1:
                    pool.wait_ge(dve_p2, NC * g + c + 1)
                    pool.wait_ge(act_cb, NCB * g + c // 2 + 1)
                    nc.gpsimd.tensor_tensor(HB[c % 3][:], HB[c % 3][:], CB[:, c, :], ALU.mult)\
                        .then_inc(pool_h, 1)

            def a_s(u, g):
                if u == 0:
                    pool.wait_ge(s_xres, 16 * (g + 1))
                    nc.gpsimd.tensor_tensor(xres[:], xres[:], bias_a[:].unsqueeze(1)
                                            .to_broadcast([P, NPAIR, E]), ALU.add).then_inc(pool_xres, 1)

            def b_xT(n, g):
                pool.wait_ge(dve_x1, NPAIR * (g + 1))
                if due(NPAIR * g):
                    pool.wait_ge(dve_x2, NPAIR * g)
                nc.gpsimd.tensor_tensor(X1b[:], X1[:], bias_b[:].unsqueeze(1)
                                        .to_broadcast([P, NPAIR, E]), ALU.add).then_inc(pool_x1b, 1)

            does = {"a_s": a_s, "b_xT": b_xT,
                    "a_ln": lambda n, g: power(0, g), "b_ln": lambda n, g: power(1, g),
                    "c_ln": lambda n, g: power(2, g), "b_kbd": b_kbd, "c_gu": c_gu}

            def walk(step, n, g):
                if step == "a_s" and n == 0 and isinstance(g, int) and g == 0:
                    pool.wait_ge(s_w, 16 * N_W)
                    pool.wait_ge(dve_bias, 2)
                if step in does:
                    does[step](n, g)
                if step == "a_ln" and isinstance(g, int) and g == 0:
                    nc.gpsimd.memset(V[:], 0.0).then_inc(pool_w, 1)

            nc.gpsimd.memset(half[:], -0.5).then_inc(pool_w, 1)
            nc.gpsimd.memset(Vc[:], 0.0).then_inc(pool_w, 1)
            nc.gpsimd.memset(comb3[:], 0.0).then_inc(pool_w, 1)
            pool.wait_ge(pool_w, 3)
            for h2 in range(2):
                rows = slice(64 * h2, 64 * h2 + 64)
                nc.gpsimd.memset(Vc[rows, :, h2:h2 + 1], 1.0).then_inc(pool_w, 1)
                nc.gpsimd.memset(Vc[rows, :, E + 2 + h2:E + 3 + h2], 1.0).then_inc(pool_w, 1)
            pool.wait_ge(pool_w, 7)
            run(pool, "gpsimd", walk)


def kernel(**inputs):
    import numpy as np
    import concourse.bacc as bacc
    from concourse import mybir as mb
    from concourse.bass_utils import run_bass_kernel_spmd

    a = {k: np.asarray(v) for k, v in inputs.items()}

    def heads_t(w):
        return w.reshape(H * DH, E).T

    def by_parity(w):
        return w.reshape(NJ, 2, DH, -1).transpose(3, 1, 0, 2)

    def columns(b):
        return b.reshape(NJ, P).T

    def rows(b, n=P):
        return np.tile(b.reshape(1, -1), (n, 1))

    def by_token(b, n):
        return np.tile(np.repeat(b.reshape(H, n).T, 2 * NA, 1), (P // n, 1))

    w_qk = np.stack([heads_t(a["L0_attn_Wq"]), heads_t(a["L0_attn_Wk"])], 1)
    w1 = np.concatenate([a["L0_ffn_w1"].reshape(FR, E), a["L0_ffn_ws1"]], 0).T
    w3 = np.concatenate([a["L0_ffn_w3"].reshape(FR, E), a["L0_ffn_ws3"]], 0).T
    w2 = np.zeros((NC * P, E), np.float32)
    w2[0:FR] = a["L0_ffn_w2"].transpose(0, 2, 1).reshape(FR, E)
    w2[FR:FR + NI] = a["L0_ffn_ws2"].T
    q = np.arange(P) % SEQ
    mask = np.where(np.arange(SEQ)[None, :] > q[:, None], np.float32(NEG), np.float32(0))
    sel = np.zeros((CW, (NC - 1) * P), np.float32)
    for part in range(3):
        sel[32 * part + np.arange(FR) // NI, np.arange(FR)] = 1
    given = [
        ("x", a["x"].reshape(TOKENS, E)),
        ("x_hba", a["x"].reshape(TOKENS // P, 2, H, NA, E).transpose(0, 2, 1, 3, 4).reshape(TOKENS, E)),
        ("ctx", a["ctx_1024"].reshape(TOKENS, E)),
        ("w_qk", w_qk.reshape(E, 2, 2, JU * P).transpose(0, 2, 1, 3).reshape(E, 2 * NJ * P)),
        ("w_v", by_parity(a["L0_attn_Wv"]).reshape(E, 2 * NJ * DH)),
        ("w_proj", a["L0_attn_proj"].reshape(NJ, P, E).transpose(1, 0, 2).reshape(P, NJ * E)),
        ("b_qk", np.concatenate([columns(a["L0_attn_bq"]), columns(a["L0_attn_bk"])], 1)),
        ("b_v", by_token(a["L0_attn_bv"], DH)),
        ("wc_qkvo", np.concatenate([a["L0_xattn_" + n].T for n in ("Wq", "Wk", "Wv", "Wo")], 1)),
        ("bc_qk", np.stack([a["L0_xattn_bq"], a["L0_xattn_bk"]], 1)),
        ("bc_v", by_token(a["L0_xattn_bv"], DC)), ("bc_o", rows(a["L0_xattn_bo"])),
        ("gate_w", a["L0_ffn_gate_w"].T), ("gate_b", rows(a["L0_ffn_gate_bias"])),
        ("w13", np.concatenate([w1, w3], 1)),
        ("w2", w2.reshape(NC, P, E).transpose(1, 0, 2).reshape(P, NC * E)),
        ("c_ident", np.eye(P, dtype=np.float32)), ("c_mask", np.tile(mask, (1, HU))),
        ("c_head", (np.arange(P)[:, None] // DC == np.arange(H)[None, :]).astype(np.float32)),
        ("c_sel", sel),
        ("c_lower", rows((np.arange(NE)[None, :] < np.arange(NE)[:, None]).astype(np.float32))),
    ]
    nc = bacc.Bacc("TRN2", target_bir_lowering=False, num_devices=1)
    arrays, args = {}, []
    for name, v in given:
        arrays["in_" + name] = np.ascontiguousarray(v)
        args.append(nc.dram_tensor("in_" + name, v.shape, mb.dt.from_np(v.dtype), kind="ExternalInput").ap())
    args.append(nc.dram_tensor("out_0", (TOKENS, E), mb.dt.float32, kind="ExternalOutput").ap())
    decoder_layer(nc, *args)
    r = run_bass_kernel_spmd(nc, [arrays], core_ids=[0])
    o = r.results[0]["out_0"].reshape(TOKENS // P, H, 2, NA, E).transpose(0, 2, 1, 3, 4)
    return np.ascontiguousarray(o).reshape(TOKENS // SEQ, SEQ, E)
```
